# Optimizing a Trainium2 kernel written in Bass

```python
import numpy as np
import jax
import jax.numpy as jnp

def _softmax(x, axis=-1):
    return jax.nn.softmax(x, axis=axis)

def _gelu(x):
    return jax.nn.gelu(x, approximate=True)

def _silu(x):
    return jax.nn.silu(x)

def _sigmoid(x):
    return jax.nn.sigmoid(x)

def _layernorm(x, axis=-1, eps=1e-05):
    m = jnp.mean(x, axis=axis, keepdims=True)
    v = jnp.var(x, axis=axis, keepdims=True)
    return (x - m) / jnp.sqrt(v + eps)

def _scatter_add(tgt, idx, src, axis=0):
    return tgt.at[idx].add(src)

def _segment_sum(src, seg, n):
    return jax.ops.segment_sum(src, seg, n)
kernel_name = 'mk_adj_resnorm_d2_adj_r2_579776'

def setup_inputs(seed: int=0):
    np.random.seed(seed)
    _w = jnp.asarray

    def _rec_inputs():
        import jax
        import jax.numpy as jnp
        _gk = jax.random.key(seed)
        x = 7.22e-05 + 1 * jax.random.normal(jax.random.fold_in(_gk, 1), (8, 1024, 256), jnp.float32)
        _w = (1.0 + jnp.arange(1024, dtype=jnp.float32)) ** (-0.5)
        _w = _w / _w.mean()
        _pij = jnp.clip(0.0078125 * _w[:, None] * _w[None, :], 0.0, 1.0)
        _a = jax.random.uniform(jax.random.fold_in(_gk, 2), (8, 1024, 1024)) < _pij
        _a = jnp.logical_or(_a, jnp.swapaxes(_a, -1, -2))
        _a = jnp.logical_or(_a, jnp.eye(1024, dtype=bool))
        _af = _a.astype(jnp.float32)
        _af = _af * jax.random.uniform(jax.random.fold_in(_gk, 3), (8, 1024, 1024), jnp.float32, 0.05, 1)
        adj = _af
        return (x, adj)
    x, adj = _rec_inputs()

    def _L0_gnn_setup():
        import jax, jax.numpy as jnp
        import numpy as np
        key = jax.random.key(seed)
        k1, k2, k3 = jax.random.split(key, 3)
        B, N, F, D = (8, 1024, 256, 256)
        x = jax.random.normal(k1, (B, N, F), dtype=jnp.float32)
        a = jax.random.uniform(k2, (B, N, N), dtype=jnp.float32)
        kernel = jax.random.normal(k3, (F, D), dtype=jnp.float32) * (1.0 / np.sqrt(F))
        return {'x': x, 'a': a, 'kernel': kernel}
    _L0_gnn_all = _L0_gnn_setup()
    _L0_gnn_in = {k: v for k, v in _L0_gnn_all.items() if k in ('kernel',)}
    del _L0_gnn_all

    def _L1_gnn_setup():
        import jax, jax.numpy as jnp
        import numpy as np
        EPS = 1e-06
        key = jax.random.key(seed)
        k1, k2, k3 = jax.random.split(key, 3)
        B, N, F, O = (8, 2048, 256, 256)
        x = jax.random.normal(k1, (B, N, F), dtype=jnp.float32)
        adj = jax.random.uniform(k2, (B, N, N), dtype=jnp.float32)
        W = jax.random.normal(k3, (O, 2 * F), dtype=jnp.float32) * (1.0 / np.sqrt(2 * F))
        return {'x': x, 'adj': adj, 'W': W}
    _L1_gnn_all = _L1_gnn_setup()
    _L1_gnn_in = {k: v for k, v in _L1_gnn_all.items() if k in ('W',)}
    del _L1_gnn_all
    return {'x': x, 'adj': adj, 'L0_gnn_kernel': _L0_gnn_in['kernel'], 'L1_gnn_W': _L1_gnn_in['W']}

def reference(x, adj, L0_gnn_kernel, L1_gnn_W):
    import jax
    import jax.numpy as jnp

    def _L0_gnn_ref(x, a, kernel):
        import jax, jax.numpy as jnp
        import numpy as np
        t = jnp.einsum('bnm,bmf->bnf', a, x)
        out = jnp.einsum('bnf,fd->bnd', t, kernel)
        out = jax.nn.relu(out)
        mask = (jnp.sum((x != 0).astype(jnp.float32), axis=-1, keepdims=True) > 0).astype(jnp.float32)
        return out * mask

    def _L1_gnn_ref(x, adj, W):
        import jax, jax.numpy as jnp
        import numpy as np
        EPS = 1e-06
        deg = jnp.sum(adj, axis=-1, keepdims=True)
        agg = jnp.einsum('bij,bjf->bif', adj, x) / jnp.maximum(deg, EPS)
        cat = jnp.concatenate([x, agg], axis=2)
        out = jnp.einsum('bnf,of->bno', cat, W)
        return jax.nn.relu(out)
    x = _layernorm(x + _L0_gnn_ref(x, adj, L0_gnn_kernel), axis=-1)
    x = _layernorm(x + _L1_gnn_ref(x, adj, L1_gnn_W), axis=-1)
    return x

_drawn_inputs = setup_inputs


def setup_inputs(seed=0):
    import zlib

    import numpy as np

    out = dict(_drawn_inputs(seed))
    spreads = {}
    factors = {}
    for name, (base, spread) in spreads.items():
        noise = np.random.default_rng([zlib.crc32(name.encode()), seed]).standard_normal(out[name].shape)
        drawn = base * np.exp(spread * noise) if base else spread * noise
        out[name] = jnp.asarray(drawn.astype(out[name].dtype))
    for name, factor in factors.items():
        out[name] = (out[name] * factor).astype(out[name].dtype)
    return out
```

```python
import concourse.bass as bass
from concourse import mybir
from contextlib import ExitStack

P = 128


def graph_layers(nc: bass.Bass, adjt: bass.AP, x: bass.AP, xt: bass.AP, k0: bass.AP, w1: bass.AP, out: bass.AP):
    fp32, fp16, bf16, u32 = mybir.dt.float32, mybir.dt.float16, mybir.dt.bfloat16, mybir.dt.uint32
    ALU = mybir.AluOpType
    ACT = mybir.ActivationFunctionType
    AX = mybir.AxisListType

    B, T = adjt.shape[0], adjt.shape[1]
    F = x.shape[3]
    FT = F // P
    N = T * P
    LN_EPS = 1e-5
    DEG_EPS = 1e-6
    TOP = 2.0 ** 14
    LEAST = 2.0 ** -59
    EXPONENT = 0x7F800000
    Y_DOWN = 2.0 ** -23
    X1_UP = 2.0 ** 11
    Z_DOWN = 2.0 ** -19
    HALF = T // 2

    ctx = ExitStack()
    with ctx:
        def sb(name, shape, dt=fp32):
            return ctx.enter_context(nc.sbuf_tensor(name, shape, dt))

        def ps(name, dt=fp32):
            return [ctx.enter_context(nc.psum_tensor(f"{name}{i}", [P, 512], dt)) for i in range(2)]

        def sem(name):
            return ctx.enter_context(nc.semaphore(name))

        adj_in = sb("adj_in", [P, T, T * P])
        adj_h, adj_l = sb("adj_h", [P, T, T * P], fp16), sb("adj_l", [P, T, T * P], fp16)
        x_in = sb("x_in", [P, T, F])
        xt_in = sb("xt_in", [P, FT, N])
        xt_h, xt_l = sb("xt_h", [P, FT, N], fp16), sb("xt_l", [P, FT, N], fp16)
        k_in, w_in = sb("k_in", [P, FT, F]), sb("w_in", [P, FT, 2 * F])
        k_h, k_l = sb("k_h", [P, FT, F], fp16), sb("k_l", [P, FT, F], fp16)
        w_h, w_l = sb("w_h", [P, FT, 2 * F], fp16), sb("w_l", [P, FT, 2 * F], fp16)
        ident = sb("ident", [P, P], fp16)
        y_h, y_l = sb("y_h", [P, T, F], fp16), sb("y_l", [P, T, F], fp16)
        z_h, z_l = sb("z_h", [P, T, F + 2], fp16), sb("z_l", [P, T, F], fp16)
        rel = sb("rel", [P, 2, F])
        pre0 = sb("pre0", [P, T, F])
        x1 = sb("x1", [P, T, F])
        x1_h, x1_l = sb("x1_h", [P, T, F], fp16), sb("x1_l", [P, T, F], fp16)
        x1t = sb("x1t", [P, 2, 2, FT, P], fp16)
        u = sb("u", [P, T, F])
        v = sb("v", [P, 2, F])
        pre1 = sb("pre1", [P, 2, F])
        res = sb("res", [P, T, F])
        stats = sb("stats", [P, 2, T, 6])
        moments = sb("moments", [P, 2, T, 2])
        std = sb("std", [P, 2, T])
        rstd = sb("rstd", [P, 2, T])
        eps0, eps1 = sb("eps0", [P, 1]), sb("eps1", [P, 1])
        deg = sb("deg", [P, T])
        rdeg = sb("rdeg", [P, T])
        abs_out = sb("abs_out", [P, 2, T * P], bf16)
        adj_mag, adj_top, adj_pow, adj_rec = (sb(f"adj_{n}", [P, T]) for n in ("mag", "top", "pow", "rec"))
        adj_s, adj_inv, deg_least = sb("adj_s", [P, T]), sb("adj_inv", [P, T]), sb("deg_least", [P, T])
        kw_mag, kw_top, kw_pow, kw_rec = (sb(f"kw_{n}", [P, 2]) for n in ("mag", "top", "pow", "rec"))
        kw_s, kw_inv = sb("kw_s", [P, 2]), sb("kw_inv", [P, 2])
        deg_q, deg_qe = sb("deg_q", [P, 1]), sb("deg_qe", [P, 1])
        row_mag, mask, unmask = sb("row_mag", [P, T]), sb("mask", [P, T]), sb("unmask", [P, T])
        x_mag, x_top, x_pow, x_rec = (sb(f"x_{n}", [P, 1]) for n in ("mag", "top", "pow", "rec"))
        x_s, x_inv, xk_inv = sb("x_s", [P, 1]), sb("x_inv", [P, 1]), sb("xk_inv", [P, 1])
        agg_inv = sb("agg_inv", [P, T])

        agg_ps, uz_ps, y_ps = ps("agg_ps"), ps("uz_ps"), ps("y_ps")
        tr_ps = [ctx.enter_context(nc.psum_tensor(f"tr_ps{i}", [P, 1024], fp16)) for i in range(2)]

        adj_loaded = [sem(f"adj_loaded{i}") for i in range(T)]
        x_loaded, xt_loaded, k_loaded, w_loaded = (sem(f"{n}_loaded") for n in ("x", "xt", "k", "w"))
        stored = [sem(f"stored{i}") for i in range(2)]
        ident_zero, consts = sem("ident_zero"), sem("consts")
        kw_top_ready, x_top_ready, adj_top_ready = sem("kw_top_ready"), sem("x_top_ready"), sem("adj_top_ready")
        stats_seen, mag_seen = sem("stats_seen"), sem("mag_seen")
        pre0_ready, x1l_ready = sem("pre0_ready"), sem("x1l_ready")
        y_done, agg0_done, agg1_done, tr_done, uz_done = (sem(f"{n}_done") for n in ("y", "agg0", "agg1", "tr", "uz"))
        adj_mag_ready, adjh_ready, xth_ready, kwh_ready = (sem(f"{n}_ready") for n in ("adj_mag", "adjh", "xth", "kwh"))
        yh_ready, zh_ready, u_ready, rel_ready = (sem(f"{n}_ready") for n in ("yh", "zh", "u", "rel"))
        x1h_ready, x1t_ready = sem("x1h_ready"), sem("x1t_ready")
        std_ready = [sem(f"std{n}_ready") for n in range(2)]
        kw_mag_ready, x_mag_ready, row_mag_ready = sem("kw_mag_ready"), sem("x_mag_ready"), sem("row_mag_ready")
        scale_step, kw_s_ready, x_s_ready, adj_s_ready = (sem(n) for n in ("scale_step", "kw_s_ready", "x_s_ready", "adj_s_ready"))
        mask_ready, agg_inv_ready, deg_least_ready = sem("mask_ready"), sem("agg_inv_ready"), sem("deg_least_ready")
        kwl_ready, xtl_ready, adjl_ready, yl_ready, zl_ready = (sem(f"{n}_ready") for n in ("kwl", "xtl", "adjl", "yl", "zl"))
        stats_ready = [sem(f"stats{n}_ready") for n in range(2)]
        moments_ready = [sem(f"moments{n}_ready") for n in range(2)]
        rstd_ready = [sem(f"rstd{n}_ready") for n in range(2)]
        x1_ready, deg_ready, rdeg_ready, agg1_free = sem("x1_ready"), sem("deg_ready"), sem("rdeg_ready"), sem("agg1_free")
        xk_inv_ready, unmask_ready, deg_q_ready = sem("xk_inv_ready"), sem("unmask_ready"), sem("deg_q_ready")
        pre1_ready, out_ready = sem("pre1_ready"), sem("out_ready")

        block = ctx.enter_context(nc.Block())

        @block.sync
        def _(sp):
            for h in range(2):
                sp.sem_inc(stored[h], 16)
            sp.dma_start(k_in[:], k0).then_inc(k_loaded, 16)
            sp.dma_start(w_in[:], w1).then_inc(w_loaded, 16)
            sp.dma_start(x_in[:], x[0]).then_inc(x_loaded, 16)
            sp.dma_start(xt_in[:], xt[0]).then_inc(xt_loaded, 16)
            for i in range(T):
                sp.dma_start(adj_in[:, i], adjt[0, i]).then_inc(adj_loaded[i], 16)

            def store(b):
                for h in range(2):
                    sp.wait_ge(out_ready, b * T + (h + 1) * HALF)
                    sp.dma_start(out[b, :, h * HALF:(h + 1) * HALF], res[:, h * HALF:(h + 1) * HALF]).then_inc(stored[h], 16)

            with sp.Fori(0, B - 1) as b:
                for i in range(T):
                    sp.wait_ge(adjl_ready, b * T + i + 1)
                    sp.dma_start(adj_in[:, i], adjt[b + 1, i]).then_inc(adj_loaded[i], 16)
                sp.wait_ge(xtl_ready, (b + 1) * FT)
                sp.dma_start(xt_in[:], xt[b + 1]).then_inc(xt_loaded, 16)
                sp.wait_ge(pre0_ready, (b + 1) * T)
                sp.dma_start(x_in[:], x[b + 1]).then_inc(x_loaded, 16)
                store(b)
            store(B - 1)
            for h in range(2):
                sp.wait_ge(stored[h], 16 * (B + 1))

        @block.gpsimd
        def _(pool):
            nc.gpsimd.memset(ident[:], 0.0).then_inc(ident_zero, 1)
            nc.gpsimd.memset(z_h[:, :, F:F + 2], 1.0).then_inc(consts, 1)
            nc.gpsimd.memset(eps0[:], LN_EPS / X1_UP ** 2).then_inc(consts, 1)
            nc.gpsimd.memset(eps1[:], LN_EPS * X1_UP ** 2).then_inc(consts, 1)
            pool.wait_ge(ident_zero, 1)
            nc.gpsimd.affine_select(out=ident[:], in_=ident[:], compare_op=ALU.not_equal, fill=1.0, base=0,
                                    pattern=[[-1, P]], channel_multiplier=1).then_inc(consts, 1)

            def top(dst, src, done):
                pool.sem_inc(mag_seen, 1)
                nc.gpsimd.partition_all_reduce(dst, src, P, bass.bass_isa.ReduceOp.max).then_inc(done, 1)

            def top_x(b):
                pool.wait_ge(x_mag_ready, b + 1)
                top(x_top[:], x_mag[:], x_top_ready)

            def top_adj(b):
                pool.wait_ge(adj_mag_ready, (b + 1) * T)
                top(adj_top[:], adj_mag[:], adj_top_ready)

            def split_x1(b, i):
                pool.wait_ge(x1h_ready, b * T + i + 1)
                nc.gpsimd.tensor_tensor(x1_l[:, i], x1[:, i], x1_h[:, i], ALU.subtract).then_inc(x1l_ready, 1)

            def body(b, more):
                for i in range(T):
                    pool.wait_ge(rel_ready, b * T + i + 1)
                    nc.gpsimd.tensor_tensor(pre0[:, i], rel[:, i % 2], x_in[:, i], ALU.add).then_inc(pre0_ready, 1)
                    if i >= 2:
                        split_x1(b, i - 2)
                split_x1(b, T - 2)
                split_x1(b, T - 1)
                if more:
                    top_adj(b + 1)
                    top_x(b + 1)

            pool.wait_ge(kw_mag_ready, 2)
            top(kw_top[:], kw_mag[:], kw_top_ready)
            top_x(0)
            top_adj(0)
            with pool.Fori(0, B - 1) as b:
                body(b, True)
            body(B - 1, False)

        @block.tensor
        def _(pe):
            def project_y(b, i):
                if not (isinstance(b, int) and b == 0 and i < 2):
                    pe.wait_ge(yl_ready, b * T + i - 1)
                if i == 0:
                    pe.wait_ge(xtl_ready, (b + 1) * FT)
                passes = [(xt_h, k_h), (xt_h, k_l), (xt_l, k_h)]
                for k in range(FT):
                    for n, (a, r) in enumerate(passes):
                        last = nc.tensor.matmul(y_ps[i % 2][:, 0:F], a[:, k, i * P:(i + 1) * P], r[:, k],
                                                start=(k == 0 and n == 0), stop=(k == FT - 1 and n == 2))
                last.then_inc(y_done, 1)

            def aggregate(i, high, low, wide, done, before=None):
                for k in range(T):
                    if before:
                        before(k)
                    at = slice(k * P, (k + 1) * P)
                    nc.tensor.matmul(agg_ps[i % 2][:, 0:wide], adj_h[:, i, at], high[:, k, 0:wide],
                                     start=(k == 0), stop=False)
                    nc.tensor.matmul(agg_ps[i % 2][:, 0:F], adj_h[:, i, at], low[:, k, 0:F], start=False, stop=False)
                    last = nc.tensor.matmul(agg_ps[i % 2][:, 0:wide], adj_l[:, i, at], high[:, k, 0:wide],
                                            start=False, stop=(k == T - 1))
                last.then_inc(done, 1)

            def transpose_x1(b, i):
                pe.wait_ge(x1l_ready, b * T + i + 1)
                for n, part in enumerate((x1_h, x1_l)):
                    for k in range(FT):
                        c = (n * FT + k) * P
                        last = nc.tensor.transpose(tr_ps[i % 2][:, c:c + P], part[:, i, k * P:(k + 1) * P], ident[:])
                last.then_inc(tr_done, 1)

            def project_uz(b, i):
                pe.wait_ge(x1t_ready, b * T + i + 1)
                if i >= 2:
                    pe.wait_ge(zl_ready, b * T + i - 1)
                passes = [(0, w_h), (0, w_l), (1, w_h)]
                for k in range(FT):
                    for n, (part, r) in enumerate(passes):
                        last = nc.tensor.matmul(uz_ps[i % 2][:], x1t[:, i % 2, part, k], r[:, k],
                                                start=(k == 0 and n == 0), stop=(k == FT - 1 and n == 2))
                last.then_inc(uz_done, 1)

            def body(b, more):
                for i in range(T):
                    pe.wait_ge(adjl_ready, b * T + i + 1)
                    if i < 2:
                        pe.wait_ge(agg1_free, b * T + i + 1)
                    else:
                        pe.wait_ge(rel_ready, b * T + i - 1)
                    each = (lambda k: pe.wait_ge(yl_ready, b * T + k + 1)) if i == 0 else None
                    aggregate(i, y_h, y_l, F, agg0_done, each)
                for i in range(T):
                    transpose_x1(b, i)
                    if i:
                        project_uz(b, i - 1)
                project_uz(b, T - 1)
                for i in range(T):
                    if i < 2:
                        pe.wait_ge(rel_ready, b * T + T - 1 + i)
                    else:
                        pe.wait_ge(agg1_free, b * T + i + 1)
                    each = (lambda k: pe.wait_ge(zl_ready, b * T + k + 1)) if i == 0 else None
                    aggregate(i, z_h, z_l, F + 1, agg1_done, each)
                    if more:
                        project_y(b + 1, i)

            pe.sem_inc(agg1_free, 2)
            pe.wait_ge(kwl_ready, 1)
            for i in range(T):
                project_y(0, i)
            pe.wait_ge(kwl_ready, 2)
            pe.wait_ge(consts, 4)
            with pe.Fori(0, B - 1) as b:
                body(b, True)
            body(B - 1, False)

        @block.scalar
        def _(act):
            def magnitude(b, i):
                act.wait_ge(adj_loaded[i], 16 * (b + 1))
                if not (isinstance(b, int) and i < 2):
                    act.wait_ge(adj_mag_ready, b * T + i - 1)
                nc.scalar.activation(abs_out[:, i % 2], adj_in[:, i], ACT.Abs, accum_out=adj_mag[:, i:i + 1]).then_inc(adj_mag_ready, 1)

            def split_adj(b, i, first=False):
                if i == 0:
                    act.wait_ge(adj_s_ready, b + 1)
                if not first:
                    act.wait_ge(agg1_done, (b - 1) * T + i + 1)
                nc.scalar.activation(adj_h[:, i], adj_in[:, i], ACT.Copy, scale=adj_s[:, i:i + 1]).then_inc(adjh_ready, 1)

            def split_x(b):
                act.wait_ge(x_s_ready, b + 1)
                act.wait_ge(xt_loaded, 16 * (b + 1))
                if not isinstance(b, int):
                    act.wait_ge(y_done, b * T)
                for k in range(FT):
                    nc.scalar.activation(xt_h[:, k], xt_in[:, k], ACT.Copy, scale=x_s[:]).then_inc(xth_ready, 1)

            def split_y(b, i):
                act.wait_ge(y_done, b * T + i + 1)
                nc.scalar.activation(y_h[:, i], y_ps[i % 2][:, 0:F], ACT.Copy, scale=Y_DOWN).then_inc(yh_ready, 1)

            def root(b, layer, i):
                act.wait_ge(moments_ready[layer], b * T + i + 1)
                nc.scalar.activation(std[:, layer, i:i + 1], moments[:, layer, i, 1:2], ACT.Sqrt,
                                     bias=(eps1 if layer else eps0)[:],
                                     scale=1.0 if layer else 1.0 / X1_UP ** 2).then_inc(std_ready[layer], 1)

            def split_x1(b, i):
                act.wait_ge(x1_ready, b * T + i + 1)
                nc.scalar.activation(x1_h[:, i], x1[:, i], ACT.Copy).then_inc(x1h_ready, 1)

            def take_uz(b, i):
                act.wait_ge(uz_done, b * T + i + 1)
                nc.scalar.activation(u[:, i], uz_ps[i % 2][:, 0:F], ACT.Copy, scale=kw_inv[:, 1:2]).then_inc(u_ready, 1)
                nc.scalar.activation(z_h[:, i, 0:F], uz_ps[i % 2][:, F:2 * F], ACT.Copy, scale=Z_DOWN).then_inc(zh_ready, 1)

            def body(b, more):
                for i in range(T):
                    act.wait_ge(agg0_done, b * T + i + 1)
                    if i == 0:
                        act.wait_ge(agg_inv_ready, b + 1)
                    nc.scalar.activation(rel[:, i % 2], agg_ps[i % 2][:, 0:F], ACT.Relu,
                                         scale=agg_inv[:, i:i + 1]).then_inc(rel_ready, 1)
                    if i >= 1:
                        root(b, 0, i - 1)
                    if i >= 2:
                        split_x1(b, i - 2)
                    if more:
                        magnitude(b + 1, i)
                root(b, 0, T - 1)
                split_x1(b, T - 2)
                split_x1(b, T - 1)
                for i in range(T):
                    act.wait_ge(tr_done, b * T + i + 1)
                    nc.scalar.activation(x1t[:, i % 2].rearrange("p a k m -> p (a k m)"), tr_ps[i % 2][:, 0:4 * P],
                                         ACT.Copy).then_inc(x1t_ready, 1)
                    if i:
                        take_uz(b, i - 1)
                take_uz(b, T - 1)
                if more:
                    split_x(b + 1)
                for i in range(T):
                    if more:
                        split_y(b + 1, i)
                    if i:
                        root(b, 1, i - 1)
                    if more and i:
                        split_adj(b + 1, i - 1)
                root(b, 1, T - 1)
                if more:
                    split_adj(b + 1, T - 1)

            act.wait_ge(kw_s_ready, 1)
            nc.scalar.activation(k_h[:], k_in[:], ACT.Copy, scale=kw_s[:, 0:1]).then_inc(kwh_ready, 1)
            split_x(0)
            for i in range(T):
                magnitude(0, i)
            for i in range(T):
                split_y(0, i)
            nc.scalar.activation(w_h[:], w_in[:], ACT.Copy, scale=kw_s[:, 1:2]).then_inc(kwh_ready, 1)
            for i in range(T):
                split_adj(0, i, first=True)
            act.wait_ge(consts, 4)
            with act.Fori(0, B - 1) as b:
                body(b, True)
            body(B - 1, False)

        @block.vector
        def _(dve):
            def link(ins, at):
                ins.then_inc(scale_step, 1)
                dve.wait_ge(scale_step, at)

            def scales(top, power, rec, s, inv, at, ready):
                link(nc.vector.tensor_scalar(rec, top, LEAST, None, ALU.max), at + 1)
                link(nc.vector.tensor_scalar(power.bitcast(u32), rec.bitcast(u32), EXPONENT, None, ALU.bitwise_and), at + 2)
                link(nc.vector.reciprocal(rec, power), at + 3)
                link(nc.vector.tensor_scalar(inv, power, 1.0 / TOP, None, ALU.mult), at + 4)
                nc.vector.tensor_scalar(s, rec, TOP, None, ALU.mult).then_inc(ready, 1)

            STEPS = 8
            FIRST_STEPS = 12

            def rows_of_x(b, q):
                at = slice(q * T // HALF, (q + 1) * T // HALF)
                dve.wait_ge(x_loaded, 16 * (b + 1))
                nc.vector.tensor_reduce(row_mag[:, at], x_in[:, at], AX.X, ALU.max,
                                        apply_absolute_value=True).then_inc(row_mag_ready, 1)

            def magnitude_x(b):
                dve.wait_ge(row_mag_ready, (b + 1) * HALF)
                nc.vector.tensor_reduce(x_mag[:], row_mag[:], AX.X, ALU.max).then_inc(x_mag_ready, 1)
                nc.vector.tensor_scalar(mask[:], row_mag[:], 0.0, None, ALU.is_gt).then_inc(mask_ready, 1)

            def scale_x(b, at):
                dve.wait_ge(x_top_ready, b + 1)
                scales(x_top[:], x_pow[:], x_rec[:], x_s[:], x_inv[:], at, x_s_ready)

            def scale_adj(b, at):
                dve.wait_ge(adj_top_ready, b + 1)
                scales(adj_top[:], adj_pow[:], adj_rec[:], adj_s[:], adj_inv[:], at, adj_s_ready)

            def split_x(b):
                for k in range(FT):
                    dve.wait_ge(xth_ready, b * FT + k + 1)
                    nc.vector.scalar_tensor_tensor(xt_l[:, k], xt_in[:, k], x_s[:], xt_h[:, k],
                                                   ALU.mult, ALU.subtract).then_inc(xtl_ready, 1)

            def split_adj(b, i):
                dve.wait_ge(adjh_ready, b * T + i + 1)
                nc.vector.scalar_tensor_tensor(adj_l[:, i], adj_in[:, i], adj_s[:, i:i + 1], adj_h[:, i],
                                               ALU.mult, ALU.subtract).then_inc(adjl_ready, 1)

            def split_y(b, i):
                dve.wait_ge(yh_ready, b * T + i + 1)
                nc.vector.scalar_tensor_tensor(y_l[:, i], y_ps[i % 2][:, 0:F], Y_DOWN, y_h[:, i],
                                               ALU.mult, ALU.subtract).then_inc(yl_ready, 1)

            def variance(b, layer, i, pre, pre_ready):
                dve.wait_ge(pre_ready, b * T + i + 1)
                nc.vector.bn_stats(stats[:, layer, i], pre).then_inc(stats_ready[layer], 1)
                dve.wait_ge(stats_ready[layer], b * T + i + 1)
                dve.sem_inc(stats_seen, 1)
                nc.vector.bn_aggr(moments[:, layer, i], stats[:, layer, i]).then_inc(moments_ready[layer], 1)

            def norm(b, layer, i, dst, pre, ready):
                dve.wait_ge(std_ready[layer], b * T + i + 1)
                nc.vector.reciprocal(rstd[:, layer, i:i + 1], std[:, layer, i:i + 1]).then_inc(rstd_ready[layer], 1)
                dve.wait_ge(rstd_ready[layer], b * T + i + 1)
                nc.vector.tensor_scalar(dst, pre, moments[:, layer, i, 0:1], rstd[:, layer, i:i + 1],
                                        ALU.subtract, ALU.mult).then_inc(ready, 1)

            def finish(b, i):
                dve.wait_ge(agg1_done, b * T + i + 1)
                nc.vector.tensor_scalar(deg[:, i:i + 1], agg_ps[i % 2][:, F:F + 1], deg_q[:], deg_least[:, i:i + 1],
                                        ALU.mult, ALU.max).then_inc(deg_ready, 1)
                dve.wait_ge(deg_ready, b * T + i + 1)
                nc.vector.reciprocal(rdeg[:, i:i + 1], deg[:, i:i + 1]).then_inc(rdeg_ready, 1)
                dve.wait_ge(rdeg_ready, b * T + i + 1)
                nc.vector.scalar_tensor_tensor(v[:, i % 2], agg_ps[i % 2][:, 0:F], rdeg[:, i:i + 1], u[:, i],
                                               ALU.mult, ALU.add).then_inc(agg1_free, 1)
                dve.wait_ge(agg1_free, b * T + i + 3)
                nc.vector.scalar_tensor_tensor(pre1[:, i % 2], v[:, i % 2], 0.0, x1[:, i],
                                               ALU.max, ALU.add).then_inc(pre1_ready, 1)

            def out_norm(b, i):
                if i % HALF == 0:
                    dve.wait_ge(stored[i // HALF], 16 * (b + 1))
                norm(b, 1, i, res[:, i], pre1[:, i % 2], out_ready)

            def layer_scales(b):
                nc.vector.tensor_scalar(xk_inv[:], x_inv[:], kw_inv[:, 0:1], 1.0 / Y_DOWN, ALU.mult, ALU.mult).then_inc(xk_inv_ready, 1)
                nc.vector.tensor_tensor(unmask[:], adj_inv[:], mask[:], ALU.mult).then_inc(unmask_ready, 1)
                dve.wait_ge(xk_inv_ready, b + 1)
                dve.wait_ge(unmask_ready, b + 1)
                nc.vector.tensor_scalar(agg_inv[:], unmask[:], xk_inv[:], None, ALU.mult).then_inc(agg_inv_ready, 1)

            def body(b, more):
                nc.vector.tensor_scalar(deg_least[:], adj_s[:], deg_qe[:], None, ALU.mult).then_inc(deg_least_ready, 1)
                for i in range(T):
                    variance(b, 0, i, pre0[:, i], pre0_ready)
                    if i:
                        norm(b, 0, i - 1, x1[:, i - 1], pre0[:, i - 1], x1_ready)
                norm(b, 0, T - 1, x1[:, T - 1], pre0[:, T - 1], x1_ready)
                if more:
                    scale_adj(b + 1, FIRST_STEPS + b * STEPS)
                for i in range(T):
                    dve.wait_ge(zh_ready, b * T + i + 1)
                    nc.vector.scalar_tensor_tensor(z_l[:, i], uz_ps[i % 2][:, F:2 * F], Z_DOWN, z_h[:, i, 0:F],
                                                   ALU.mult, ALU.subtract).then_inc(zl_ready, 1)
                    if more and i >= HALF:
                        rows_of_x(b + 1, i - HALF)
                if more:
                    magnitude_x(b + 1)
                    scale_x(b + 1, FIRST_STEPS + b * STEPS + STEPS // 2)
                    split_x(b + 1)
                    layer_scales(b + 1)
                for i in range(T):
                    finish(b, i)
                    variance(b, 1, i, pre1[:, i % 2], pre1_ready)
                    if more:
                        split_y(b + 1, i)
                    if i:
                        out_norm(b, i - 1)
                        if more:
                            split_adj(b + 1, i - 1)
                out_norm(b, T - 1)
                if more:
                    split_adj(b + 1, T - 1)

            dve.wait_ge(k_loaded, 16)
            nc.vector.tensor_reduce(kw_mag[:, 0:1], k_in[:], AX.XY, ALU.max, apply_absolute_value=True).then_inc(kw_mag_ready, 1)
            dve.wait_ge(w_loaded, 16)
            nc.vector.tensor_reduce(kw_mag[:, 1:2], w_in[:], AX.XY, ALU.max, apply_absolute_value=True).then_inc(kw_mag_ready, 1)
            for q in range(HALF):
                rows_of_x(0, q)
            magnitude_x(0)
            dve.wait_ge(kw_top_ready, 1)
            scales(kw_top[:], kw_pow[:], kw_rec[:], kw_s[:], kw_inv[:], 0, kw_s_ready)
            scale_x(0, 4)
            dve.wait_ge(kwh_ready, 1)
            nc.vector.scalar_tensor_tensor(k_l[:], k_in[:], kw_s[:, 0:1], k_h[:], ALU.mult, ALU.subtract).then_inc(kwl_ready, 1)
            split_x(0)
            scale_adj(0, 8)
            layer_scales(0)
            for i in range(T):
                split_y(0, i)
            dve.wait_ge(kwh_ready, 2)
            nc.vector.scalar_tensor_tensor(w_l[:], w_in[:], kw_s[:, 1:2], w_h[:], ALU.mult, ALU.subtract).then_inc(kwl_ready, 1)
            nc.vector.tensor_scalar(deg_q[:], kw_s[:, 1:2], Z_DOWN, None, ALU.mult).then_inc(deg_q_ready, 1)
            nc.vector.tensor_scalar(deg_qe[:], kw_s[:, 1:2], Z_DOWN * DEG_EPS, None, ALU.mult).then_inc(deg_q_ready, 1)
            dve.wait_ge(deg_q_ready, 2)
            for i in range(T):
                split_adj(0, i)
            with dve.Fori(0, B - 1) as b:
                body(b, True)
            body(B - 1, False)


def kernel(x, adj, L0_gnn_kernel, L1_gnn_W):
    import numpy as np
    import concourse.bacc as bacc
    from concourse.bass_utils import run_bass_kernel_spmd

    x, adj, k0, w1 = (np.asarray(a) for a in (x, adj, L0_gnn_kernel, L1_gnn_W))
    B, N, F = x.shape
    T, FT = N // P, F // P
    arrays = {
        "adjt": adj.reshape(B, T, P, T, P).transpose(0, 1, 4, 3, 2).reshape(B, T, P, T * P),
        "x": x.reshape(B, T, P, F).transpose(0, 2, 1, 3),
        "xt": x.reshape(B, N, FT, P).transpose(0, 3, 2, 1),
        "k0": k0.reshape(FT, P, F).transpose(1, 0, 2),
        "w1": w1.reshape(F, 2, FT, P).transpose(3, 2, 1, 0).reshape(P, FT, 2 * F),
    }
    arrays = {n: np.ascontiguousarray(a) for n, a in arrays.items()}
    nc = bacc.Bacc("TRN2", target_bir_lowering=False, num_devices=1)
    aps = {n: nc.dram_tensor(n, a.shape, mybir.dt.from_np(a.dtype), kind="ExternalInput").ap() for n, a in arrays.items()}
    out = nc.dram_tensor("out", (B, P, T, F), mybir.dt.float32, kind="ExternalOutput").ap()
    graph_layers(nc, aps["adjt"], aps["x"], aps["xt"], aps["k0"], aps["w1"], out)
    result = run_bass_kernel_spmd(nc, [arrays], core_ids=[0]).results[0]["out"]
    return np.ascontiguousarray(result.transpose(0, 2, 1, 3)).reshape(B, N, F)
```

```python
import concourse.bass as bass
from concourse import mybir
from contextlib import ExitStack

P = 128


def graph_layers(nc: bass.Bass, adjt: bass.AP, x: bass.AP, xt: bass.AP, k0: bass.AP, w1: bass.AP, out: bass.AP):
    fp32, fp16, bf16, u32 = mybir.dt.float32, mybir.dt.float16, mybir.dt.bfloat16, mybir.dt.uint32
    ALU = mybir.AluOpType
    ACT = mybir.ActivationFunctionType
    AX = mybir.AxisListType

    B, T = adjt.shape[0], adjt.shape[1]
    F = x.shape[3]
    FT = F // P
    N = T * P
    LN_EPS = 1e-5
    DEG_EPS = 1e-6
    TOP = 2.0 ** 14
    LEAST = 2.0 ** -59
    EXPONENT = 0x7F800000
    Y_DOWN = 2.0 ** -23
    X1_UP = 2.0 ** 11
    Z_DOWN = 2.0 ** -19
    HALF = T // 2
    AHEAD = 2
    ROWS = [(0,), (1, 2), (3, 4), (5, 6), (7,)] + [()] * 3
    MAGS = [(), (0,), (1,), (2, 3), (4,), (5,), (6,), (7,)]
    SPLITS = {3: 0, 5: 1}
    LATE = range(1, 4)

    ctx = ExitStack()
    with ctx:
        def sb(name, shape, dt=fp32):
            return ctx.enter_context(nc.sbuf_tensor(name, shape, dt))

        def ps(name, dt=fp32):
            return [ctx.enter_context(nc.psum_tensor(f"{name}{i}", [P, 512], dt)) for i in range(2)]

        def sem(name):
            return ctx.enter_context(nc.semaphore(name))

        adj_in = sb("adj_in", [P, T, T * P])
        adj_h, adj_l = sb("adj_h", [P, T, T * P], fp16), sb("adj_l", [P, T, T * P], fp16)
        x_in = sb("x_in", [P, T, F])
        xt_in = sb("xt_in", [P, FT, N])
        xt_h, xt_l = sb("xt_h", [P, FT, N], fp16), sb("xt_l", [P, FT, N], fp16)
        k_in, w_in = sb("k_in", [P, FT, F]), sb("w_in", [P, FT, 2 * F])
        k_h, k_l = sb("k_h", [P, FT, F], fp16), sb("k_l", [P, FT, F], fp16)
        w_h, w_l = sb("w_h", [P, FT, 2 * F], fp16), sb("w_l", [P, FT, 2 * F], fp16)
        ident = sb("ident", [P, P], fp16)
        y_h, y_l = sb("y_h", [P, T, F], fp16), sb("y_l", [P, T, F], fp16)
        z_h, z_l = sb("z_h", [P, T, F + 2], fp16), sb("z_l", [P, T, F], fp16)
        rel = sb("rel", [P, 2, F])
        pre0 = sb("pre0", [P, T, F])
        x1 = sb("x1", [P, T, F])
        x1_h, x1_l = sb("x1_h", [P, T, F], fp16), sb("x1_l", [P, T, F], fp16)
        x1t = sb("x1t", [P, 2, 2, FT, P], fp16)
        u = sb("u", [P, T, F])
        v = sb("v", [P, 2, F])
        pre1 = sb("pre1", [P, 2, F])
        res = sb("res", [P, T, F])
        stats = sb("stats", [P, 2, T, 6])
        moments = sb("moments", [P, 2, T, 2])
        std = sb("std", [P, 2, T])
        rstd = sb("rstd", [P, 2, T])
        eps0, eps1 = sb("eps0", [P, 1]), sb("eps1", [P, 1])
        root_first = sb("root_first", [P, 1])
        deg = sb("deg", [P, T])
        rdeg = sb("rdeg", [P, T])
        abs_out = sb("abs_out", [P, 2, T * P], bf16)
        data_mag, data_top, data_pow, data_rec = (sb(f"data_{n}", [P, T + 1]) for n in ("mag", "top", "pow", "rec"))
        data_s, data_inv = sb("data_s", [P, T + 1]), sb("data_inv", [P, T + 1])
        x_s, x_inv = data_s[:, T:T + 1], data_inv[:, T:T + 1]
        deg_least = sb("deg_least", [P, T])
        kw_mag, kw_top, kw_pow, kw_rec = (sb(f"kw_{n}", [P, 2]) for n in ("mag", "top", "pow", "rec"))
        kw_s, kw_inv = sb("kw_s", [P, 2]), sb("kw_inv", [P, 2])
        abs_row = sb("abs_row", [P, 2, F], bf16)
        deg_q, deg_qe = sb("deg_q", [P, 1]), sb("deg_qe", [P, 1])
        row_mag, mask, unmask = sb("row_mag", [P, T]), sb("mask", [P, T]), sb("unmask", [P, T])
        xt_mag, xk_inv = sb("xt_mag", [P, 2 * FT]), sb("xk_inv", [P, 1])
        agg_inv = sb("agg_inv", [P, T])

        agg_ps, uz_ps, y_ps = ps("agg_ps"), ps("uz_ps"), ps("y_ps")
        tr_ps = [ctx.enter_context(nc.psum_tensor(f"tr_ps{i}", [P, 1024], fp16)) for i in range(2)]

        adj_loaded = [sem(f"adj_loaded{i}") for i in range(T)]
        x_loaded, xt_loaded, k_loaded, w_loaded = (sem(f"{n}_loaded") for n in ("x", "xt", "k", "w"))
        xt0_loaded = [sem(f"xt0_loaded{k}") for k in range(FT)]
        stored = [sem(f"stored{i}") for i in range(2)]
        ident_zero, consts = sem("ident_zero"), sem("consts")
        kw_top_ready, first_top_ready, data_top_ready = sem("kw_top_ready"), sem("first_top_ready"), sem("data_top_ready")
        stats_seen, mag_seen = sem("stats_seen"), sem("mag_seen")
        pre0_ready, x1l_ready = sem("pre0_ready"), sem("x1l_ready")
        y_done, agg0_done, agg1_done, tr_done, uz_done = (sem(f"{n}_done") for n in ("y", "agg0", "agg1", "tr", "uz"))
        adj_mag_ready, adjh_ready, xth_ready, kwh_ready = (sem(f"{n}_ready") for n in ("adj_mag", "adjh", "xth", "kwh"))
        yh_ready, zh_ready, u_ready, rel_ready = (sem(f"{n}_ready") for n in ("yh", "zh", "u", "rel"))
        x1h_ready, x1t_ready = sem("x1h_ready"), sem("x1t_ready")
        std_ready = [sem(f"std{n}_ready") for n in range(2)]
        kw_mag_ready, x_mag_ready, row_mag_ready = sem("kw_mag_ready"), sem("x_mag_ready"), sem("row_mag_ready")
        xt_mag_ready = sem("xt_mag_ready")
        scale_step, kw_s_ready, data_s_ready = sem("scale_step"), sem("kw_s_ready"), sem("data_s_ready")
        first_s_ready, first_mag_ready = sem("first_s_ready"), sem("first_mag_ready")
        mask_ready, agg_inv_ready, deg_least_ready = sem("mask_ready"), sem("agg_inv_ready"), sem("deg_least_ready")
        kwl_ready, xtl_ready, adjl_ready, yl_ready, zl_ready = (sem(f"{n}_ready") for n in ("kwl", "xtl", "adjl", "yl", "zl"))
        stats_ready = [sem(f"stats{n}_ready") for n in range(2)]
        moments_ready = [sem(f"moments{n}_ready") for n in range(2)]
        rstd_ready = [sem(f"rstd{n}_ready") for n in range(2)]
        x1_ready, deg_ready, rdeg_ready, agg1_free = sem("x1_ready"), sem("deg_ready"), sem("rdeg_ready"), sem("agg1_free")
        xk_inv_ready, unmask_ready, deg_q_ready = sem("xk_inv_ready"), sem("unmask_ready"), sem("deg_q_ready")
        pre1_ready, out_ready = sem("pre1_ready"), sem("out_ready")

        block = ctx.enter_context(nc.Block())

        @block.sync
        def _(sp):
            for h in range(2):
                sp.sem_inc(stored[h], 16)
            sp.dma_start(k_in[:], k0).then_inc(k_loaded, 16)
            for k in range(FT):
                sp.dma_start(xt_in[:, k], xt[0, :, k]).then_inc(xt0_loaded[k], 16)
            for i in range(T):
                sp.dma_start(adj_in[:, i], adjt[0, i]).then_inc(adj_loaded[i], 16)
                if i == HALF - 1:
                    sp.dma_start(w_in[:], w1).then_inc(w_loaded, 16)
            sp.dma_start(x_in[:], x[0]).then_inc(x_loaded, 16)

            def load_adj(b, i):
                sp.wait_ge(adjl_ready, (b - 1) * T + i + 1)
                sp.dma_start(adj_in[:, i], adjt[b, i]).then_inc(adj_loaded[i], 16)

            def store_last(b):
                sp.wait_ge(out_ready, (b + 1) * T)
                sp.dma_start(out[b, :, HALF:T], res[:, HALF:T]).then_inc(stored[1], 16)

            with sp.Fori(0, B - 1) as b:
                for i in range(AHEAD):
                    load_adj(b + 1, i)
                sp.wait_ge(xtl_ready, (b + 1) * FT)
                sp.dma_start(xt_in[:], xt[b + 1]).then_inc(xt_loaded, 16)
                for i in range(AHEAD, T):
                    load_adj(b + 1, i)
                sp.wait_ge(pre0_ready, (b + 1) * T)
                sp.dma_start(x_in[:], x[b + 1]).then_inc(x_loaded, 16)
                store_last(b)
            store_last(B - 1)
            for h in range(2):
                sp.wait_ge(stored[h], 16 * (B + 1))

        @block.gpsimd
        def _(pool):
            nc.gpsimd.memset(ident[:], 0.0).then_inc(ident_zero, 1)
            nc.gpsimd.memset(z_h[:, :, F:F + 2], 1.0).then_inc(consts, 1)
            nc.gpsimd.memset(eps0[:], LN_EPS / X1_UP ** 2).then_inc(consts, 1)
            nc.gpsimd.memset(eps1[:], LN_EPS * X1_UP ** 2).then_inc(consts, 1)
            pool.wait_ge(ident_zero, 1)
            nc.gpsimd.affine_select(out=ident[:], in_=ident[:], compare_op=ALU.not_equal, fill=1.0, base=0,
                                    pattern=[[-1, P]], channel_multiplier=1).then_inc(consts, 1)

            def top(dst, src, done):
                pool.sem_inc(mag_seen, 1)
                nc.gpsimd.partition_all_reduce(dst, src, P, bass.bass_isa.ReduceOp.max).then_inc(done, 1)

            def top_data(b):
                pool.wait_ge(adj_mag_ready, b * T + HALF)
                pool.wait_ge(x_mag_ready, b + 1)
                top(data_top[:], data_mag[:], data_top_ready)

            def top_first(at):
                top(data_top[:, at], data_mag[:, at], first_top_ready)

            def split_x1(b, i):
                pool.wait_ge(x1h_ready, b * T + i + 1)
                nc.gpsimd.tensor_tensor(x1_l[:, i], x1[:, i], x1_h[:, i], ALU.subtract).then_inc(x1l_ready, 1)

            def body(b, more):
                for i in range(T):
                    pool.wait_ge(rel_ready, b * T + i + 1)
                    nc.gpsimd.tensor_tensor(pre0[:, i], rel[:, i % 2], x_in[:, i], ALU.add).then_inc(pre0_ready, 1)
                    if i in LATE:
                        split_x1(b, i - 1)
                    if i + 1 not in LATE:
                        split_x1(b, i)
                if more:
                    top_data(b + 1)

            pool.wait_ge(kw_mag_ready, 1)
            top(kw_top[:, 0:1], kw_mag[:, 0:1], kw_top_ready)
            pool.wait_ge(x_mag_ready, 1)
            top_first(slice(T, T + 1))
            pool.wait_ge(adj_mag_ready, HALF)
            top_first(slice(0, HALF))
            pool.wait_ge(first_mag_ready, T - HALF)
            top_first(slice(HALF, T))
            pool.wait_ge(kw_mag_ready, 2)
            top(kw_top[:, 1:2], kw_mag[:, 1:2], kw_top_ready)
            with pool.Fori(0, B - 1) as b:
                body(b, True)
            body(B - 1, False)

        @block.tensor
        def _(pe):
            def project_y(b, i):
                if not (isinstance(b, int) and b == 0 and i < 2):
                    pe.wait_ge(yl_ready, b * T + i - 1)
                if i == 0:
                    pe.wait_ge(xtl_ready, (b + 1) * FT)
                passes = [(xt_h, k_h), (xt_h, k_l), (xt_l, k_h)]
                for k in range(FT):
                    for n, (a, r) in enumerate(passes):
                        last = nc.tensor.matmul(y_ps[i % 2][:, 0:F], a[:, k, i * P:(i + 1) * P], r[:, k],
                                                start=(k == 0 and n == 0), stop=(k == FT - 1 and n == 2))
                last.then_inc(y_done, 1)

            def aggregate(i, high, low, wide, done, ks=range(T), parts_ready=None, count=0):
                for k in ks:
                    if parts_ready is not None:
                        pe.wait_ge(parts_ready, count + k + 1)
                    at = slice(k * P, (k + 1) * P)
                    nc.tensor.matmul(agg_ps[i % 2][:, 0:wide], adj_h[:, i, at], high[:, k, 0:wide],
                                     start=(k == 0), stop=False)
                    nc.tensor.matmul(agg_ps[i % 2][:, 0:F], adj_h[:, i, at], low[:, k, 0:F], start=False, stop=False)
                    last = nc.tensor.matmul(agg_ps[i % 2][:, 0:wide], adj_l[:, i, at], high[:, k, 0:wide],
                                            start=False, stop=(k == T - 1))
                if k == T - 1:
                    last.then_inc(done, 1)

            def transpose_x1(b, i):
                pe.wait_ge(x1l_ready, b * T + i + 1)
                for n, part in enumerate((x1_h, x1_l)):
                    for k in range(FT):
                        c = (n * FT + k) * P
                        last = nc.tensor.transpose(tr_ps[i % 2][:, c:c + P], part[:, i, k * P:(k + 1) * P], ident[:])
                last.then_inc(tr_done, 1)

            def project_uz(b, i):
                pe.wait_ge(x1t_ready, b * T + i + 1)
                if i == 0:
                    pe.wait_ge(kwl_ready, 2)
                if i >= 2:
                    pe.wait_ge(zl_ready, b * T + i - 1)
                passes = [(0, w_h), (0, w_l), (1, w_h)]
                for k in range(FT):
                    for n, (part, r) in enumerate(passes):
                        last = nc.tensor.matmul(uz_ps[i % 2][:], x1t[:, i % 2, part, k], r[:, k],
                                                start=(k == 0 and n == 0), stop=(k == FT - 1 and n == 2))
                last.then_inc(uz_done, 1)

            def layer0(b, i):
                pe.wait_ge(adjl_ready, b * T + i + 1)
                if i < 2:
                    pe.wait_ge(agg1_free, b * T + i + 1)
                else:
                    pe.wait_ge(rel_ready, b * T + i - 1)
                if i == 0:
                    aggregate(i, y_h, y_l, F, agg0_done, parts_ready=yl_ready, count=b * T)
                else:
                    aggregate(i, y_h, y_l, F, agg0_done)

            def layer1(b, i):
                if i < 2:
                    pe.wait_ge(rel_ready, b * T + T - 1 + i)
                else:
                    pe.wait_ge(agg1_free, b * T + i + 1)
                aggregate(i, z_h, z_l, F + 1, agg1_done)

            def body(b, more):
                for i in range(T):
                    layer0(b, i)
                    if i >= 2:
                        transpose_x1(b, i - 2)
                    if i >= 3:
                        project_uz(b, i - 3)
                transpose_x1(b, T - 2)
                project_uz(b, T - 3)
                project_uz(b, T - 2)
                transpose_x1(b, T - 1)
                pe.wait_ge(rel_ready, b * T + T - 1)
                aggregate(0, z_h, z_l, F + 1, agg1_done, range(HALF), parts_ready=zl_ready, count=b * T)
                project_uz(b, T - 1)
                aggregate(0, z_h, z_l, F + 1, agg1_done, range(HALF, T), parts_ready=zl_ready, count=b * T)
                for i in range(1, T):
                    layer1(b, i)
                    if more:
                        project_y(b + 1, i - 1)
                if more:
                    project_y(b + 1, T - 1)

            pe.sem_inc(agg1_free, 2)
            pe.wait_ge(kwl_ready, 1)
            for i in range(T):
                project_y(0, i)
            pe.wait_ge(consts, 4)
            with pe.Fori(0, B - 1) as b:
                body(b, True)
            body(B - 1, False)

        @block.scalar
        def _(act):
            def magnitude(b, i):
                act.wait_ge(adj_loaded[i], 16 * (b + 1))
                if not isinstance(b, int):
                    act.wait_ge(adj_mag_ready, (b - 1) * T + HALF + i - 1)
                elif i >= 2:
                    act.wait_ge(adj_mag_ready, i - 1)
                nc.scalar.activation(abs_out[:, i % 2], adj_in[:, i], ACT.Abs, accum_out=data_mag[:, i:i + 1]).then_inc(adj_mag_ready, 1)

            def split_adj(b, i, first=False):
                if not first:
                    act.wait_ge(agg1_done, (b - 1) * T + i + 1)
                nc.scalar.activation(adj_h[:, i], adj_in[:, i], ACT.Copy, scale=data_s[:, i:i + 1]).then_inc(adjh_ready, 1)

            def split_x(b, k):
                if k == 0 and not isinstance(b, int):
                    act.wait_ge(data_s_ready, b)
                    act.wait_ge(y_done, b * T)
                nc.scalar.activation(xt_h[:, k], xt_in[:, k], ACT.Copy, scale=x_s).then_inc(xth_ready, 1)

            def split_y(b, i):
                act.wait_ge(y_done, b * T + i + 1)
                nc.scalar.activation(y_h[:, i], y_ps[i % 2][:, 0:F], ACT.Copy, scale=Y_DOWN).then_inc(yh_ready, 1)

            def root(b, layer, i):
                act.wait_ge(moments_ready[layer], b * T + i + 1)
                nc.scalar.activation(std[:, layer, i:i + 1], moments[:, layer, i, 1:2], ACT.Sqrt,
                                     bias=(eps1 if layer else eps0)[:],
                                     scale=1.0 if layer else 1.0 / X1_UP ** 2).then_inc(std_ready[layer], 1)

            def split_x1(b, i):
                act.wait_ge(x1_ready, b * T + i + 1)
                nc.scalar.activation(x1_h[:, i], x1[:, i], ACT.Copy).then_inc(x1h_ready, 1)

            def row_sum(b, i):
                act.wait_ge(x_loaded, 16 * (b + 1))
                act.wait_ge(row_mag_ready, b * T + i - 1)
                nc.scalar.activation(abs_row[:, i % 2], x_in[:, i], ACT.Abs, accum_out=row_mag[:, i:i + 1]).then_inc(row_mag_ready, 1)

            def take_x1t(b, i):
                act.wait_ge(tr_done, b * T + i + 1)
                nc.scalar.activation(x1t[:, i % 2].rearrange("p a k m -> p (a k m)"), tr_ps[i % 2][:, 0:4 * P],
                                     ACT.Copy).then_inc(x1t_ready, 1)

            def take_uz(b, i):
                act.wait_ge(uz_done, b * T + i + 1)
                nc.scalar.activation(u[:, i], uz_ps[i % 2][:, 0:F], ACT.Copy, scale=kw_inv[:, 1:2]).then_inc(u_ready, 1)
                nc.scalar.activation(z_h[:, i, 0:F], uz_ps[i % 2][:, F:2 * F], ACT.Copy, scale=Z_DOWN).then_inc(zh_ready, 1)

            def store_first(b):
                act.wait_ge(out_ready, b * T + HALF)
                act.dma_start(out[b, :, 0:HALF], res[:, 0:HALF]).then_inc(stored[0], 16)

            def body(b, more):
                for i in range(T):
                    act.wait_ge(agg0_done, b * T + i + 1)
                    if i == 0:
                        act.wait_ge(agg_inv_ready, b + 1)
                    nc.scalar.activation(rel[:, i % 2], agg_ps[i % 2][:, 0:F], ACT.Relu,
                                         scale=agg_inv[:, i:i + 1]).then_inc(rel_ready, 1)
                    if i in LATE:
                        split_x1(b, i - 1)
                    if i >= 2:
                        take_x1t(b, i - 2)
                    if i >= 3:
                        take_uz(b, i - 3)
                    root(b, 0, i)
                    if i == T - 1:
                        take_x1t(b, T - 2)
                    elif more:
                        for t in MAGS[i]:
                            magnitude(b + 1, t)
                    if i + 1 not in LATE:
                        split_x1(b, i)
                if more:
                    for t in MAGS[T - 1]:
                        magnitude(b + 1, t)
                take_uz(b, T - 3)
                take_uz(b, T - 2)
                take_x1t(b, T - 1)
                if more:
                    split_x(b + 1, 0)
                take_uz(b, T - 1)
                if more:
                    split_x(b + 1, 1)
                for i in range(T):
                    if i >= 1:
                        root(b, 1, i - 1)
                    if more:
                        if i:
                            split_y(b + 1, i - 1)
                        if i == T - 1:
                            split_y(b + 1, i)
                        split_adj(b + 1, i)
                        for t in ROWS[i]:
                            row_sum(b + 1, t)
                    if i == T - 2:
                        store_first(b)
                root(b, 1, T - 1)

            act.wait_ge(consts, 4)
            nc.scalar.activation(root_first[:], eps0[:], ACT.Sqrt)
            act.wait_ge(kw_s_ready, 1)
            nc.scalar.activation(k_h[:], k_in[:], ACT.Copy, scale=kw_s[:, 0:1]).then_inc(kwh_ready, 1)
            act.wait_ge(first_s_ready, 1)
            for k in range(FT):
                split_x(0, k)
            for i in range(HALF):
                magnitude(0, i)
                split_y(0, i)
            act.wait_ge(first_s_ready, 2)
            split_adj(0, 0, first=True)
            for i in range(HALF, T):
                split_y(0, i)
            for i in range(1, HALF):
                split_adj(0, i, first=True)
            act.wait_ge(first_s_ready, 3)
            split_adj(0, HALF, first=True)
            act.wait_ge(kw_s_ready, 2)
            nc.scalar.activation(w_h[:], w_in[:], ACT.Copy, scale=kw_s[:, 1:2]).then_inc(kwh_ready, 1)
            for i in range(HALF + 1, T):
                split_adj(0, i, first=True)
            with act.Fori(0, B - 1) as b:
                body(b, True)
            body(B - 1, False)

        @block.vector
        def _(dve):
            def link(ins, at):
                ins.then_inc(scale_step, 1)
                dve.wait_ge(scale_step, at)

            def scales(top, power, rec, s, inv, at, ready):
                link(nc.vector.tensor_scalar(rec, top, LEAST, None, ALU.max), at + 1)
                link(nc.vector.tensor_scalar(power.bitcast(u32), rec.bitcast(u32), EXPONENT, None, ALU.bitwise_and), at + 2)
                link(nc.vector.reciprocal(rec, power), at + 3)
                link(nc.vector.tensor_scalar(inv, power, 1.0 / TOP, None, ALU.mult), at + 4)
                nc.vector.tensor_scalar(s, rec, TOP, None, ALU.mult).then_inc(ready, 1)

            STEPS = 4
            FIRST = 5

            def magnitude_x(b, q):
                if isinstance(b, int):
                    dve.wait_ge(xt0_loaded[q // 2], 16)
                else:
                    dve.wait_ge(xt_loaded, 16 * b)
                nc.vector.tensor_reduce(xt_mag[:, q:q + 1], xt_in[:, q // 2, q % 2 * N // 2:(q % 2 + 1) * N // 2], AX.X, ALU.max,
                                        apply_absolute_value=True).then_inc(xt_mag_ready, 1)

            def join_magnitude_x(b):
                dve.wait_ge(xt_mag_ready, (b + 1) * 2 * FT)
                nc.vector.tensor_reduce(data_mag[:, T:T + 1], xt_mag[:], AX.X, ALU.max).then_inc(x_mag_ready, 1)

            def scale_data(b):
                dve.wait_ge(data_top_ready, b)
                scales(data_top[:], data_pow[:], data_rec[:], data_s[:], data_inv[:], (FIRST + b - 1) * STEPS, data_s_ready)

            def scale_kw(n):
                at = slice(n, n + 1)
                dve.wait_ge(kw_top_ready, n + 1)
                scales(kw_top[:, at], kw_pow[:, at], kw_rec[:, at], kw_s[:, at], kw_inv[:, at], (0, 4)[n] * STEPS, kw_s_ready)

            def scale_first(n, at):
                order = (1, 2, 3)[n]
                dve.wait_ge(first_top_ready, n + 1)
                scales(data_top[:, at], data_pow[:, at], data_rec[:, at], data_s[:, at], data_inv[:, at], order * STEPS, first_s_ready)

            def split_x(b, k):
                dve.wait_ge(xth_ready, b * FT + k + 1)
                nc.vector.scalar_tensor_tensor(xt_l[:, k], xt_in[:, k], x_s, xt_h[:, k],
                                               ALU.mult, ALU.subtract).then_inc(xtl_ready, 1)

            def split_adj(b, i):
                dve.wait_ge(adjh_ready, b * T + i + 1)
                nc.vector.scalar_tensor_tensor(adj_l[:, i], adj_in[:, i], data_s[:, i:i + 1], adj_h[:, i],
                                               ALU.mult, ALU.subtract).then_inc(adjl_ready, 1)

            def split_y(b, i):
                dve.wait_ge(yh_ready, b * T + i + 1)
                nc.vector.scalar_tensor_tensor(y_l[:, i], y_ps[i % 2][:, 0:F], Y_DOWN, y_h[:, i],
                                               ALU.mult, ALU.subtract).then_inc(yl_ready, 1)

            def sums(b, layer, i):
                dve.wait_ge((pre0_ready, pre1_ready)[layer], b * T + i + 1)
                nc.vector.bn_stats(stats[:, layer, i], pre1[:, i % 2] if layer else pre0[:, i]).then_inc(stats_ready[layer], 1)

            def variance(b, layer, i):
                dve.wait_ge(stats_ready[layer], b * T + i + 1)
                dve.sem_inc(stats_seen, 1)
                nc.vector.bn_aggr(moments[:, layer, i], stats[:, layer, i]).then_inc(moments_ready[layer], 1)

            def inverse_root(b, layer, i):
                dve.wait_ge(std_ready[layer], b * T + i + 1)
                nc.vector.reciprocal(rstd[:, layer, i:i + 1], std[:, layer, i:i + 1]).then_inc(rstd_ready[layer], 1)

            def norm(b, layer, i):
                dve.wait_ge(rstd_ready[layer], b * T + i + 1)
                if layer and i % HALF == 0:
                    dve.wait_ge(stored[i // HALF], 16 * (b + 1))
                dst, pre, ready = (res[:, i], pre1[:, i % 2], out_ready) if layer else (x1[:, i], pre0[:, i], x1_ready)
                nc.vector.tensor_scalar(dst, pre, moments[:, layer, i, 0:1], rstd[:, layer, i:i + 1],
                                        ALU.subtract, ALU.mult).then_inc(ready, 1)

            def degree(b, i):
                dve.wait_ge(agg1_done, b * T + i + 1)
                nc.vector.tensor_scalar(deg[:, i:i + 1], agg_ps[i % 2][:, F:F + 1], deg_q[:], deg_least[:, i:i + 1],
                                        ALU.mult, ALU.max).then_inc(deg_ready, 1)
                dve.wait_ge(deg_ready, b * T + i + 1)
                nc.vector.reciprocal(rdeg[:, i:i + 1], deg[:, i:i + 1]).then_inc(rdeg_ready, 1)

            def divide(b, i):
                dve.wait_ge(rdeg_ready, b * T + i + 1)
                nc.vector.scalar_tensor_tensor(v[:, i % 2], agg_ps[i % 2][:, 0:F], rdeg[:, i:i + 1], u[:, i],
                                               ALU.mult, ALU.add).then_inc(agg1_free, 1)

            def residual(b, i):
                dve.wait_ge(agg1_free, 2 + b * T + i + 1)
                nc.vector.scalar_tensor_tensor(pre1[:, i % 2], v[:, i % 2], 0.0, x1[:, i],
                                               ALU.max, ALU.add).then_inc(pre1_ready, 1)

            def layer_scales(b):
                dve.wait_ge(row_mag_ready, (b + 1) * T)
                nc.vector.tensor_scalar(mask[:], row_mag[:], 0.0, None, ALU.is_gt).then_inc(mask_ready, 1)
                nc.vector.tensor_scalar(xk_inv[:], x_inv, kw_inv[:, 0:1], 1.0 / Y_DOWN, ALU.mult, ALU.mult).then_inc(xk_inv_ready, 1)
                dve.wait_ge(mask_ready, b + 1)
                nc.vector.tensor_tensor(unmask[:], data_inv[:, 0:T], mask[:], ALU.mult).then_inc(unmask_ready, 1)
                dve.wait_ge(xk_inv_ready, b + 1)
                dve.wait_ge(unmask_ready, b + 1)
                nc.vector.tensor_scalar(agg_inv[:], unmask[:], xk_inv[:], None, ALU.mult).then_inc(agg_inv_ready, 1)

            def split_z(b, i):
                dve.wait_ge(zh_ready, b * T + i + 1)
                nc.vector.scalar_tensor_tensor(z_l[:, i], uz_ps[i % 2][:, F:2 * F], Z_DOWN, z_h[:, i, 0:F],
                                               ALU.mult, ALU.subtract).then_inc(zl_ready, 1)

            def body(b, more):
                nc.vector.tensor_scalar(deg_least[:], data_s[:, 0:T], deg_qe[:], None, ALU.mult).then_inc(deg_least_ready, 1)
                for i in range(T):
                    if i + AHEAD < T:
                        split_adj(b, i + AHEAD)
                    sums(b, 0, i)
                    variance(b, 0, i)
                    if i >= 3:
                        split_z(b, i - 3)
                    inverse_root(b, 0, i)
                    norm(b, 0, i)
                    if more and i >= HALF:
                        magnitude_x(b + 1, i - HALF)
                    if more and i == T - 1:
                        join_magnitude_x(b + 1)
                split_z(b, T - 3)
                if more:
                    scale_data(b + 1)
                split_z(b, T - 2)
                split_z(b, T - 1)
                if more:
                    for k in range(FT):
                        split_x(b + 1, k)
                for i in range(T):
                    degree(b, i)
                    divide(b, i)
                    if i:
                        inverse_root(b, 1, i - 1)
                    residual(b, i)
                    if i:
                        norm(b, 1, i - 1)
                    if more and i:
                        split_y(b + 1, i - 1)
                    sums(b, 1, i)
                    if more:
                        if i == T - 2:
                            layer_scales(b + 1)
                        if i == T - 1:
                            split_y(b + 1, i)
                    variance(b, 1, i)
                    if more and i in SPLITS:
                        split_adj(b + 1, SPLITS[i])
                inverse_root(b, 1, T - 1)
                norm(b, 1, T - 1)

            dve.wait_ge(k_loaded, 16)
            nc.vector.tensor_reduce(kw_mag[:, 0:1], k_in[:], AX.XY, ALU.max, apply_absolute_value=True).then_inc(kw_mag_ready, 1)
            scale_kw(0)
            for q in range(2 * FT):
                magnitude_x(0, q)
            join_magnitude_x(0)
            dve.wait_ge(kwh_ready, 1)
            nc.vector.scalar_tensor_tensor(k_l[:], k_in[:], kw_s[:, 0:1], k_h[:], ALU.mult, ALU.subtract).then_inc(kwl_ready, 1)
            scale_first(0, slice(T, T + 1))
            for k in range(FT):
                split_x(0, k)
            for i in range(HALF):
                split_y(0, i)
            scale_first(1, slice(0, HALF))
            split_adj(0, 0)
            for i in range(HALF, T):
                split_y(0, i)
            for i in range(HALF, T):
                dve.wait_ge(adj_loaded[i], 16)
                nc.vector.tensor_reduce(data_mag[:, i:i + 1], adj_in[:, i], AX.X, ALU.max,
                                        apply_absolute_value=True).then_inc(first_mag_ready, 1)
            split_adj(0, 1)
            scale_first(2, slice(HALF, T))
            dve.wait_ge(w_loaded, 16)
            nc.vector.tensor_reduce(kw_mag[:, 1:2], w_in[:], AX.XY, ALU.max, apply_absolute_value=True).then_inc(kw_mag_ready, 1)
            dve.wait_ge(x_loaded, 16)
            nc.vector.tensor_reduce(row_mag[:], x_in[:], AX.X, ALU.max, apply_absolute_value=True).then_inc(row_mag_ready, T)
            layer_scales(0)
            scale_kw(1)
            dve.wait_ge(kw_s_ready, 2)
            nc.vector.tensor_scalar(deg_q[:], kw_s[:, 1:2], Z_DOWN, None, ALU.mult).then_inc(deg_q_ready, 1)
            nc.vector.tensor_scalar(deg_qe[:], kw_s[:, 1:2], Z_DOWN * DEG_EPS, None, ALU.mult).then_inc(deg_q_ready, 1)
            dve.wait_ge(kwh_ready, 2)
            nc.vector.scalar_tensor_tensor(w_l[:], w_in[:], kw_s[:, 1:2], w_h[:], ALU.mult, ALU.subtract).then_inc(kwl_ready, 1)
            dve.wait_ge(deg_q_ready, 2)
            with dve.Fori(0, B - 1) as b:
                body(b, True)
            body(B - 1, False)


def kernel(x, adj, L0_gnn_kernel, L1_gnn_W):
    import numpy as np
    import concourse.bacc as bacc
    from concourse.bass_utils import run_bass_kernel_spmd

    x, adj, k0, w1 = (np.asarray(a) for a in (x, adj, L0_gnn_kernel, L1_gnn_W))
    B, N, F = x.shape
    T, FT = N // P, F // P
    arrays = {
        "adjt": adj.reshape(B, T, P, T, P).transpose(0, 1, 4, 3, 2).reshape(B, T, P, T * P),
        "x": x.reshape(B, T, P, F).transpose(0, 2, 1, 3),
        "xt": x.reshape(B, N, FT, P).transpose(0, 3, 2, 1),
        "k0": k0.reshape(FT, P, F).transpose(1, 0, 2),
        "w1": w1.reshape(F, 2, FT, P).transpose(3, 2, 1, 0).reshape(P, FT, 2 * F),
    }
    arrays = {n: np.ascontiguousarray(a) for n, a in arrays.items()}
    nc = bacc.Bacc("TRN2", target_bir_lowering=False, num_devices=1)
    aps = {n: nc.dram_tensor(n, a.shape, mybir.dt.from_np(a.dtype), kind="ExternalInput").ap() for n, a in arrays.items()}
    out = nc.dram_tensor("out", (B, P, T, F), mybir.dt.float32, kind="ExternalOutput").ap()
    graph_layers(nc, aps["adjt"], aps["x"], aps["xt"], aps["k0"], aps["w1"], out)
    result = run_bass_kernel_spmd(nc, [arrays], core_ids=[0]).results[0]["out"]
    return np.ascontiguousarray(result.transpose(0, 2, 1, 3)).reshape(B, N, F)
```

```python
import concourse.bass as bass
from concourse import mybir
from contextlib import ExitStack

P = 128


def graph_layers(nc: bass.Bass, adjt: bass.AP, x: bass.AP, xt: bass.AP, k0: bass.AP, w1: bass.AP, out: bass.AP):
    fp32, fp16, bf16, u32 = mybir.dt.float32, mybir.dt.float16, mybir.dt.bfloat16, mybir.dt.uint32
    ALU = mybir.AluOpType
    ACT = mybir.ActivationFunctionType
    AX = mybir.AxisListType

    B, T = adjt.shape[0], adjt.shape[1]
    F = x.shape[3]
    FT = F // P
    N = T * P
    LN_EPS = 1e-5
    DEG_EPS = 1e-6
    TOP = 2.0 ** 14
    LEAST = 2.0 ** -59
    EXPONENT = 0x7F800000
    Y_DOWN = 2.0 ** -23
    X1_UP = 2.0 ** 11
    Z_DOWN = 2.0 ** -19
    HALF = T // 2
    assert T == 8 and B >= 3

    SUMS_EARLY = [(), (0,), (1,), (), (), (), (7,), ()]
    SUMS_LATE = [(), (), (2,), (3,), (4, 5), (6,), (), ()]
    PROJECTS = [(), (0,), (1,), (2,), (3,), (4, 5), (6, 7), ()]
    SPLITS = {1: 0, 3: 1, 5: 2}
    ROWS = [(0,), (1, 2), (3, 4), (5, 6), (7,), (), (), ()]
    AHEAD = len(SPLITS)
    X_FROM = 3
    LATE = range(1, 4)

    FIRST_SUMS, FIRST_MAXIMA = (0, 2, 3, 5), (1, 4, 6, 7)
    FIRST_ROWS = HALF
    OF_K_CHAIN, OF_X_CHAIN, LOW_CHAIN, HIGH_CHAIN, OF_W_CHAIN, BEFORE = range(6)

    ctx = ExitStack()
    with ctx:
        def sb(name, shape, dt=fp32):
            return ctx.enter_context(nc.sbuf_tensor(name, shape, dt))

        def ps(name, dt=fp32, wide=512):
            return [ctx.enter_context(nc.psum_tensor(f"{name}{i}", [P, wide], dt)) for i in range(2)]

        def sem(name):
            return ctx.enter_context(nc.semaphore(name))

        adj_in = sb("adj_in", [P, T, T * P])
        adj_h, adj_l = sb("adj_h", [P, T, T * P], fp16), sb("adj_l", [P, T, T * P], fp16)
        x_in = sb("x_in", [P, T, F])
        xt_in = sb("xt_in", [P, FT, N])
        xt_h, xt_l = sb("xt_h", [P, FT, N], fp16), sb("xt_l", [P, FT, N], fp16)
        k_in, w_in = sb("k_in", [P, FT, F]), sb("w_in", [P, FT, 2 * F])
        k_h, k_l = sb("k_h", [P, FT, F], fp16), sb("k_l", [P, FT, F], fp16)
        w_h, w_l = sb("w_h", [P, FT, 2 * F], fp16), sb("w_l", [P, FT, 2 * F], fp16)
        ident = sb("ident", [P, P], fp16)
        y_h, y_l = sb("y_h", [P, T, F], fp16), sb("y_l", [P, T, F], fp16)
        z_h, z_l = sb("z_h", [P, T, F + 2], fp16), sb("z_l", [P, T, F], fp16)
        rel = sb("rel", [P, 2, F])
        pre0 = sb("pre0", [P, T, F])
        x1 = sb("x1", [P, T, F])
        x1_h, x1_l = sb("x1_h", [P, T, F], fp16), sb("x1_l", [P, T, F], fp16)
        x1t = sb("x1t", [P, 2, 2, FT, P], fp16)
        u = sb("u", [P, T, F])
        v = sb("v", [P, 2, F])
        pre1 = sb("pre1", [P, 2, F])
        res = sb("res", [P, T, F])
        stats = sb("stats", [P, 2, T, 6])
        moments = sb("moments", [P, 2, T, 2])
        std = sb("std", [P, 2, T])
        rstd = sb("rstd", [P, 2, T])
        eps0, eps1 = sb("eps0", [P, 1]), sb("eps1", [P, 1])
        root_first = sb("root_first", [P, 1])
        deg = sb("deg", [P, T])
        rdeg = sb("rdeg", [P, T])
        OF_X, OF_A, OF_W, OF_K = 0, 1, T + 1, T + 2
        mag, top, power, rec, scale, inv = (sb(n, [P, T + 3]) for n in ("mag", "top", "power", "rec", "scale", "inv"))

        def of(tile, first, count=1):
            return tile[:, first:first + count]

        x_s, k_s, w_s = of(scale, OF_X), of(scale, OF_K), of(scale, OF_W)
        deg_least = sb("deg_least", [P, T])
        abs_adj, abs_quarter = sb("abs_adj", [P, 2, T * P], bf16), sb("abs_quarter", [P, N // 2], bf16)
        abs_row, abs_w = sb("abs_row", [P, 2, F], bf16), sb("abs_w", [P, FT, 2 * F], bf16)
        deg_q, deg_qe = sb("deg_q", [P, 1]), sb("deg_qe", [P, 1])
        row_mag, mask, unmask = sb("row_mag", [P, T]), sb("mask", [P, T]), sb("unmask", [P, T])
        xt_mag, xk_inv = sb("xt_mag", [P, 2 * FT]), sb("xk_inv", [P, 1])
        agg_inv = sb("agg_inv", [P, T])

        agg_ps, uz_ps, y_ps = ps("agg_ps"), ps("uz_ps"), ps("y_ps")
        tr_ps = ps("tr_ps", fp16, 1024)
        y_banks = y_ps + uz_ps

        def x_half(tile, half):
            return tile[:, :, half * N // 2:(half + 1) * N // 2]

        def is_first(b):
            return isinstance(b, int) and b == 0


        adj_loaded = [sem(f"adj_loaded{i}") for i in range(T)]
        x_loaded, xt_loaded, k_loaded, w_loaded = (sem(f"{n}_loaded") for n in ("x", "xt", "k", "w"))
        xt0_loaded = [sem(f"xt0_loaded{k}") for k in range(FT)]
        stored = [sem(f"stored{i}") for i in range(2)]
        ident_zero, consts = sem("ident_zero"), sem("consts")
        top_ready, mag_seen = sem("top_ready"), sem("mag_seen")
        pre0_ready, x1l_ready = sem("pre0_ready"), sem("x1l_ready")
        y_done, agg0_done, agg1_done, tr_done, uz_done = (sem(f"{n}_done") for n in ("y", "agg0", "agg1", "tr", "uz"))
        adj_mag_ready, adjh_ready, xth_ready, kwh_ready = (sem(f"{n}_ready") for n in ("adj_mag", "adjh", "xth", "kwh"))
        yh_ready, zh_ready, u_ready, rel_ready = (sem(f"{n}_ready") for n in ("yh", "zh", "u", "rel"))
        xt_quarter_ready, row_sum_ready, w_mag_ready = sem("xt_quarter_ready"), sem("row_sum_ready"), sem("w_mag_ready")
        x1h_ready, x1t_ready = sem("x1h_ready"), sem("x1t_ready")
        std_ready = [sem(f"std{n}_ready") for n in range(2)]
        k_mag_ready, x_mag_ready, row_mag_ready = sem("k_mag_ready"), sem("x_mag_ready"), sem("row_mag_ready")
        xt_mag_ready, first_mag_ready = sem("xt_mag_ready"), sem("first_mag_ready")
        scale_step, scale_ready = sem("scale_step"), sem("scale_ready")
        mask_ready, agg_inv_ready, deg_least_ready = sem("mask_ready"), sem("agg_inv_ready"), sem("deg_least_ready")
        kwl_ready, xtl_ready, adjl_ready, yl_ready, zl_ready = (sem(f"{n}_ready") for n in ("kwl", "xtl", "adjl", "yl", "zl"))
        stats_ready = [sem(f"stats{n}_ready") for n in range(2)]
        moments_ready = [sem(f"moments{n}_ready") for n in range(2)]
        rstd_ready = [sem(f"rstd{n}_ready") for n in range(2)]
        x1_ready, deg_ready, rdeg_ready, agg1_free = sem("x1_ready"), sem("deg_ready"), sem("rdeg_ready"), sem("agg1_free")
        xk_inv_ready, unmask_ready, deg_q_ready = sem("xk_inv_ready"), sem("unmask_ready"), sem("deg_q_ready")
        pre1_ready, out_ready, stats_seen = sem("pre1_ready"), sem("out_ready"), sem("stats_seen")

        block = ctx.enter_context(nc.Block())

        @block.sync
        def _(sp):
            for half_stored in stored:
                sp.sem_inc(half_stored, 16)
            sp.dma_start(k_in[:], k0).then_inc(k_loaded, 16)
            for k in range(FT):
                sp.dma_start(xt_in[:, k], xt[0, :, k]).then_inc(xt0_loaded[k], 16)
            for i in range(T):
                sp.dma_start(adj_in[:, i], adjt[0, i]).then_inc(adj_loaded[i], 16)
            sp.dma_start(x_in[:], x[0]).then_inc(x_loaded, 16)
            sp.dma_start(w_in[:], w1).then_inc(w_loaded, 16)

            def load_adj(b, i):
                sp.wait_ge(adjl_ready, (b - 1) * T + i + 1)
                sp.dma_start(adj_in[:, i], adjt[b, i]).then_inc(adj_loaded[i], 16)

            def store_last(b):
                sp.wait_ge(out_ready, (b + 1) * T)
                sp.dma_start(out[b, :, HALF:T], res[:, HALF:T]).then_inc(stored[1], 16)

            def body(b, more):
                sp.wait_ge(xtl_ready, (b + 1) * 2)
                sp.dma_start(xt_in[:], xt[b + 1]).then_inc(xt_loaded, 16)
                for i in range(AHEAD, T):
                    load_adj(b + 1, i)
                sp.wait_ge(pre0_ready, (b + 1) * T)
                sp.dma_start(x_in[:], x[b + 1]).then_inc(x_loaded, 16)
                if more:
                    for i in range(AHEAD):
                        load_adj(b + 2, i)
                store_last(b)

            for i in range(AHEAD):
                load_adj(1, i)
            with sp.Fori(0, B - 2) as b:
                body(b, True)
            body(B - 2, False)
            for first, end in ((HALF, T - 1), (T - 1, T)):
                sp.wait_ge(out_ready, (B - 1) * T + end)
                sp.dma_start(out[B - 1, :, first:end], res[:, first:end]).then_inc(stored[1], 16)
            sp.wait_ge(stored[0], 16 * (B + 1))
            sp.wait_ge(stored[1], 16 * (B + 2))

        @block.gpsimd
        def _(pool):
            nc.gpsimd.memset(ident[:], 0.0).then_inc(ident_zero, 1)
            nc.gpsimd.memset(z_h[:, :, F:F + 2], 1.0).then_inc(consts, 1)
            nc.gpsimd.memset(eps0[:], LN_EPS / X1_UP ** 2).then_inc(consts, 1)
            nc.gpsimd.memset(eps1[:], LN_EPS * X1_UP ** 2).then_inc(consts, 1)
            pool.wait_ge(ident_zero, 1)
            nc.gpsimd.affine_select(out=ident[:], in_=ident[:], compare_op=ALU.not_equal, fill=1.0, base=0,
                                    pattern=[[-1, P]], channel_multiplier=1).then_inc(consts, 1)

            def largest(first, count=1):
                pool.sem_inc(mag_seen, 1)
                nc.gpsimd.partition_all_reduce(of(top, first, count), of(mag, first, count), P,
                                               bass.bass_isa.ReduceOp.max).then_inc(top_ready, 1)

            def largest_data(b):
                pool.wait_ge(adj_mag_ready, (b - 1) * T + len(FIRST_SUMS) + T)
                pool.wait_ge(x_mag_ready, b + 1)
                largest(OF_X, 1 + T)

            def split_x1(b, i):
                pool.wait_ge(x1h_ready, b * T + i + 1)
                nc.gpsimd.tensor_tensor(x1_l[:, i], x1[:, i], x1_h[:, i], ALU.subtract).then_inc(x1l_ready, 1)

            def body(b, more):
                for i in range(T):
                    if more and i == T - 1:
                        largest_data(b + 1)
                    pool.wait_ge(rel_ready, b * T + i + 1)
                    nc.gpsimd.tensor_tensor(pre0[:, i], rel[:, i % 2], x_in[:, i], ALU.add).then_inc(pre0_ready, 1)
                    if i in LATE:
                        split_x1(b, i - 1)
                    if i + 1 not in LATE:
                        split_x1(b, i)

            pool.wait_ge(k_mag_ready, 1)
            largest(OF_K)
            pool.wait_ge(x_mag_ready, 1)
            largest(OF_X)
            pool.wait_ge(adj_mag_ready, sum(i < HALF for i in FIRST_SUMS))
            pool.wait_ge(first_mag_ready, sum(i < HALF for i in FIRST_MAXIMA))
            largest(OF_A, HALF)
            pool.wait_ge(adj_mag_ready, len(FIRST_SUMS))
            pool.wait_ge(first_mag_ready, len(FIRST_MAXIMA))
            largest(OF_A + HALF, HALF)
            pool.wait_ge(w_mag_ready, 1)
            largest(OF_W)
            with pool.Fori(0, B - 1) as b:
                body(b, True)
            body(B - 1, False)

        @block.tensor
        def _(pe):
            def project_y(b, i):
                bank = y_banks[i % len(y_banks)]
                if not (is_first(b) and i < len(y_banks)):
                    pe.wait_ge(yl_ready, b * T + i + 1 - len(y_banks))
                if i % HALF == 0:
                    pe.wait_ge(xtl_ready, 2 * b + i // HALF + 1)
                passes = [(xt_h, k_h), (xt_h, k_l), (xt_l, k_h)]
                for k in range(FT):
                    for n, (a, r) in enumerate(passes):
                        last = nc.tensor.matmul(bank[:, 0:F], a[:, k, i * P:(i + 1) * P], r[:, k],
                                                start=(k == 0 and n == 0), stop=(k == FT - 1 and n == 2))
                last.then_inc(y_done, 1)

            def aggregate(i, high, low, wide, done, ks=range(T), parts_ready=None, count=0):
                for k in ks:
                    if parts_ready is not None:
                        pe.wait_ge(parts_ready, count + k + 1)
                    at = slice(k * P, (k + 1) * P)
                    nc.tensor.matmul(agg_ps[i % 2][:, 0:wide], adj_h[:, i, at], high[:, k, 0:wide],
                                     start=(k == 0), stop=False)
                    nc.tensor.matmul(agg_ps[i % 2][:, 0:F], adj_h[:, i, at], low[:, k, 0:F], start=False, stop=False)
                    last = nc.tensor.matmul(agg_ps[i % 2][:, 0:wide], adj_l[:, i, at], high[:, k, 0:wide],
                                            start=False, stop=(k == T - 1))
                if k == T - 1:
                    last.then_inc(done, 1)

            def transpose_x1(b, i):
                pe.wait_ge(x1l_ready, b * T + i + 1)
                for n, part in enumerate((x1_h, x1_l)):
                    for k in range(FT):
                        c = (n * FT + k) * P
                        last = nc.tensor.transpose(tr_ps[i % 2][:, c:c + P], part[:, i, k * P:(k + 1) * P], ident[:])
                last.then_inc(tr_done, 1)

            def project_uz(b, i):
                pe.wait_ge(x1t_ready, b * T + i + 1)
                if i == 0:
                    pe.wait_ge(kwl_ready, 2)
                if i >= 2:
                    pe.wait_ge(zl_ready, b * T + i - 1)
                passes = [(0, w_h), (0, w_l), (1, w_h)]
                for k in range(FT):
                    for n, (part, r) in enumerate(passes):
                        last = nc.tensor.matmul(uz_ps[i % 2][:], x1t[:, i % 2, part, k], r[:, k],
                                                start=(k == 0 and n == 0), stop=(k == FT - 1 and n == 2))
                last.then_inc(uz_done, 1)

            def layer0(b, i):
                pe.wait_ge(adjl_ready, b * T + i + 1)
                if i < 2:
                    pe.wait_ge(agg1_free, b * T + i + 1)
                else:
                    pe.wait_ge(rel_ready, b * T + i - 1)
                if i == 0:
                    aggregate(i, y_h, y_l, F, agg0_done, parts_ready=yl_ready, count=b * T)
                else:
                    aggregate(i, y_h, y_l, F, agg0_done)

            def layer1_part(b, i, first, end):
                aggregate(i, z_h, z_l, F + 1, agg1_done, range(first, end), parts_ready=zl_ready, count=b * T)

            def layer1_parts(b, first, end):
                for i in range(2):
                    layer1_part(b, i, first, end)

            def layer1(b, i):
                pe.wait_ge(agg1_free, b * T + i + 1)
                aggregate(i, z_h, z_l, F + 1, agg1_done)

            def body(b, more):
                for i in range(T):
                    layer0(b, i)
                    if i >= 2:
                        transpose_x1(b, i - 2)
                    if i >= 3:
                        project_uz(b, i - 3)
                pe.wait_ge(rel_ready, b * T + T - 1)
                layer1_part(b, 0, 0, HALF)
                transpose_x1(b, T - 2)
                project_uz(b, T - 3)
                pe.wait_ge(rel_ready, b * T + T)
                layer1_part(b, 1, 0, HALF)
                transpose_x1(b, T - 1)
                project_uz(b, T - 2)
                layer1_parts(b, HALF, HALF + 1)
                project_uz(b, T - 1)
                layer1_parts(b, HALF + 1, T - 1)
                layer1_parts(b, T - 1, T)
                for i in range(1, T):
                    if i >= 2:
                        layer1(b, i)
                    if more:
                        for t in PROJECTS[i]:
                            project_y(b + 1, t)

            pe.sem_inc(agg1_free, 2)
            pe.wait_ge(kwl_ready, 1)
            for i in range(T):
                project_y(0, i)
            pe.wait_ge(consts, 4)
            with pe.Fori(0, B - 1) as b:
                body(b, True)
            body(B - 1, False)

        @block.scalar
        def _(act):
            def magnitude(b, i, n, before):
                act.wait_ge(adj_loaded[i], 16 * (b + 1))
                if not (is_first(b) and n < 2):
                    act.wait_ge(adj_mag_ready, before + n - 1)
                nc.scalar.activation(abs_adj[:, n % 2], adj_in[:, i], ACT.Abs, accum_out=of(mag, OF_A + i)).then_inc(adj_mag_ready, 1)

            def magnitude_first(i):
                magnitude(0, i, FIRST_SUMS.index(i), 0)

            def magnitude_next(b, i):
                magnitude(b, i, i, (b - 1) * T + len(FIRST_SUMS))

            def split_adj(b, i):
                if not is_first(b):
                    act.wait_ge(agg1_done, (b - 1) * T + i + 1)
                nc.scalar.activation(adj_h[:, i], adj_in[:, i], ACT.Copy, scale=of(scale, OF_A + i)).then_inc(adjh_ready, 1)

            def split_x(b, half):
                if half == 0 and not is_first(b):
                    act.wait_ge(scale_ready, BEFORE + b)
                    act.wait_ge(y_done, b * T)
                nc.scalar.activation(x_half(xt_h, half), x_half(xt_in, half), ACT.Copy, scale=x_s).then_inc(xth_ready, 1)

            def split_y(b, i):
                act.wait_ge(y_done, b * T + i + 1)
                nc.scalar.activation(y_h[:, i], y_banks[i % len(y_banks)][:, 0:F], ACT.Copy, scale=Y_DOWN).then_inc(yh_ready, 1)

            def root(b, layer, i):
                act.wait_ge(moments_ready[layer], b * T + i + 1)
                nc.scalar.activation(std[:, layer, i:i + 1], moments[:, layer, i, 1:2], ACT.Sqrt,
                                     bias=(eps1 if layer else eps0)[:],
                                     scale=1.0 if layer else 1.0 / X1_UP ** 2).then_inc(std_ready[layer], 1)

            def split_x1(b, i):
                act.wait_ge(x1_ready, b * T + i + 1)
                nc.scalar.activation(x1_h[:, i], x1[:, i], ACT.Copy).then_inc(x1h_ready, 1)

            def row_sum(b, i):
                act.wait_ge(x_loaded, 16 * (b + 1))
                before = 0 if is_first(b) else (b - 1) * T + FIRST_ROWS
                if not (is_first(b) and i < 2):
                    act.wait_ge(row_sum_ready, before + i - 1)
                nc.scalar.activation(abs_row[:, i % 2], x_in[:, i], ACT.Abs, accum_out=row_mag[:, i:i + 1]).then_inc(row_sum_ready, 1)

            def take_x1t(b, i):
                act.wait_ge(tr_done, b * T + i + 1)
                nc.scalar.activation(x1t[:, i % 2].rearrange("p a k m -> p (a k m)"), tr_ps[i % 2][:, 0:4 * P],
                                     ACT.Copy).then_inc(x1t_ready, 1)

            def take_uz(b, i):
                act.wait_ge(uz_done, b * T + i + 1)
                nc.scalar.activation(u[:, i], uz_ps[i % 2][:, 0:F], ACT.Copy, scale=of(inv, OF_W)).then_inc(u_ready, 1)
                nc.scalar.activation(z_h[:, i, 0:F], uz_ps[i % 2][:, F:2 * F], ACT.Copy, scale=Z_DOWN).then_inc(zh_ready, 1)

            def store_first(b):
                act.wait_ge(out_ready, b * T + HALF)
                act.dma_start(out[b, :, 0:HALF], res[:, 0:HALF]).then_inc(stored[0], 16)

            def relu(b, i):
                act.wait_ge(agg0_done, b * T + i + 1)
                if i == 0:
                    act.wait_ge(agg_inv_ready, b + 1)
                nc.scalar.activation(rel[:, i % 2], agg_ps[i % 2][:, 0:F], ACT.Relu,
                                     scale=agg_inv[:, i:i + 1]).then_inc(rel_ready, 1)

            def body(b, more):
                for i in range(T):
                    if i:
                        relu(b, i)
                    if i in LATE:
                        split_x1(b, i - 1)
                    if i >= 2:
                        take_x1t(b, i - 2)
                    if i >= 3:
                        take_uz(b, i - 3)
                    if more:
                        for t in SUMS_EARLY[i]:
                            magnitude_next(b + 1, t)
                    root(b, 0, i)
                    if more:
                        for t in SUMS_LATE[i]:
                            magnitude_next(b + 1, t)
                    if i == T - 1:
                        take_x1t(b, T - 2)
                    if i + 1 not in LATE:
                        split_x1(b, i)
                take_uz(b, T - 3)
                if more:
                    split_x(b + 1, 0)
                take_x1t(b, T - 1)
                take_uz(b, T - 2)
                take_uz(b, T - 1)
                if more:
                    split_x(b + 1, 1)
                for i in range(T):
                    if i >= 1:
                        root(b, 1, i - 1)
                    if more:
                        for t in PROJECTS[i]:
                            split_y(b + 1, t)
                        split_adj(b + 1, i)
                        for t in ROWS[i]:
                            row_sum(b + 1, t)
                    if i == T - 2:
                        store_first(b)
                if more:
                    relu(b + 1, 0)
                root(b, 1, T - 1)

            act.wait_ge(consts, 4)
            nc.scalar.activation(root_first[:], eps0[:], ACT.Sqrt)
            act.wait_ge(scale_ready, OF_K_CHAIN + 1)
            nc.scalar.activation(k_h[:], k_in[:], ACT.Copy, scale=k_s).then_inc(kwh_ready, 1)
            act.wait_ge(xt0_loaded[FT - 1], 16)
            nc.scalar.activation(abs_quarter[:], xt_in[:, FT - 1, N // 2:N], ACT.Abs,
                                 accum_out=xt_mag[:, 2 * FT - 1:2 * FT]).then_inc(xt_quarter_ready, 1)
            magnitude_first(0)
            act.wait_ge(scale_ready, OF_X_CHAIN + 1)
            split_x(0, 0)
            split_x(0, 1)
            magnitude_first(2)
            magnitude_first(3)
            split_y(0, 0)
            split_y(0, 1)
            act.wait_ge(scale_ready, LOW_CHAIN + 1)
            split_adj(0, 0)
            split_y(0, 2)
            split_y(0, 3)
            magnitude_first(5)
            split_y(0, 4)
            split_y(0, 5)
            split_adj(0, 1)
            split_y(0, 6)
            split_y(0, 7)
            split_adj(0, 2)
            for i in range(FIRST_ROWS):
                row_sum(0, i)
            split_adj(0, 3)
            act.wait_ge(w_loaded, 16)
            nc.scalar.activation(abs_w[:], w_in[:], ACT.Abs, accum_out=of(mag, OF_W)).then_inc(w_mag_ready, 1)
            act.wait_ge(scale_ready, HIGH_CHAIN + 1)
            split_adj(0, 4)
            relu(0, 0)
            split_adj(0, 5)
            act.wait_ge(scale_ready, OF_W_CHAIN + 1)
            nc.scalar.activation(w_h[:], w_in[:], ACT.Copy, scale=w_s).then_inc(kwh_ready, 1)
            split_adj(0, 6)
            split_adj(0, 7)
            with act.Fori(0, B - 1) as b:
                body(b, True)
            body(B - 1, False)

        @block.vector
        def _(dve):
            STEPS = 4

            def link(ins, at):
                ins.then_inc(scale_step, 1)
                dve.wait_ge(scale_step, at)

            def scales(n, first, count=1):
                dve.wait_ge(top_ready, n + 1)
                t, p, r = (of(tile, first, count) for tile in (top, power, rec))
                at = n * STEPS
                link(nc.vector.tensor_scalar(r, t, LEAST, None, ALU.max), at + 1)
                link(nc.vector.tensor_scalar(p.bitcast(u32), r.bitcast(u32), EXPONENT, None, ALU.bitwise_and), at + 2)
                link(nc.vector.reciprocal(r, p), at + 3)
                link(nc.vector.tensor_scalar(of(inv, first, count), p, 1.0 / TOP, None, ALU.mult), at + 4)
                nc.vector.tensor_scalar(of(scale, first, count), r, TOP, None, ALU.mult).then_inc(scale_ready, 1)

            def magnitude_first(i):
                dve.wait_ge(adj_loaded[i], 16)
                nc.vector.tensor_reduce(of(mag, OF_A + i), adj_in[:, i], AX.X, ALU.max,
                                        apply_absolute_value=True).then_inc(first_mag_ready, 1)

            def magnitude_x(b, q):
                if is_first(b):
                    dve.wait_ge(xt0_loaded[q // 2], 16)
                else:
                    dve.wait_ge(xt_loaded, 16 * b)
                nc.vector.tensor_reduce(xt_mag[:, q:q + 1], xt_in[:, q // 2, q % 2 * N // 2:(q % 2 + 1) * N // 2], AX.X, ALU.max,
                                        apply_absolute_value=True).then_inc(xt_mag_ready, 1)

            def join_magnitude_x(b):
                dve.wait_ge(xt_mag_ready, (b + 1) * 2 * FT - 1)
                nc.vector.tensor_reduce(of(mag, OF_X), xt_mag[:], AX.X, ALU.max).then_inc(x_mag_ready, 1)

            def split_x(b, half):
                dve.wait_ge(xth_ready, 2 * b + half + 1)
                nc.vector.scalar_tensor_tensor(x_half(xt_l, half), x_half(xt_in, half), x_s, x_half(xt_h, half),
                                               ALU.mult, ALU.subtract).then_inc(xtl_ready, 1)

            def split_adj(b, i):
                dve.wait_ge(adjh_ready, b * T + i + 1)
                nc.vector.scalar_tensor_tensor(adj_l[:, i], adj_in[:, i], of(scale, OF_A + i), adj_h[:, i],
                                               ALU.mult, ALU.subtract).then_inc(adjl_ready, 1)

            def split_y(b, i):
                dve.wait_ge(yh_ready, b * T + i + 1)
                nc.vector.scalar_tensor_tensor(y_l[:, i], y_banks[i % len(y_banks)][:, 0:F], Y_DOWN, y_h[:, i],
                                               ALU.mult, ALU.subtract).then_inc(yl_ready, 1)

            def sums(b, layer, i):
                dve.wait_ge((pre0_ready, pre1_ready)[layer], b * T + i + 1)
                nc.vector.bn_stats(stats[:, layer, i], pre1[:, i % 2] if layer else pre0[:, i]).then_inc(stats_ready[layer], 1)

            def variance(b, layer, i):
                dve.wait_ge(stats_ready[layer], b * T + i + 1)
                dve.sem_inc(stats_seen, 1)
                nc.vector.bn_aggr(moments[:, layer, i], stats[:, layer, i]).then_inc(moments_ready[layer], 1)

            def inverse_root(b, layer, i):
                dve.wait_ge(std_ready[layer], b * T + i + 1)
                nc.vector.reciprocal(rstd[:, layer, i:i + 1], std[:, layer, i:i + 1]).then_inc(rstd_ready[layer], 1)

            def norm(b, layer, i):
                dve.wait_ge(rstd_ready[layer], b * T + i + 1)
                if layer and i % HALF == 0:
                    dve.wait_ge(stored[i // HALF], 16 * (b + 1))
                dst, pre, ready = (res[:, i], pre1[:, i % 2], out_ready) if layer else (x1[:, i], pre0[:, i], x1_ready)
                nc.vector.tensor_scalar(dst, pre, moments[:, layer, i, 0:1], rstd[:, layer, i:i + 1],
                                        ALU.subtract, ALU.mult).then_inc(ready, 1)

            def degree(b, i):
                dve.wait_ge(agg1_done, b * T + i + 1)
                nc.vector.tensor_scalar(deg[:, i:i + 1], agg_ps[i % 2][:, F:F + 1], deg_q[:], deg_least[:, i:i + 1],
                                        ALU.mult, ALU.max).then_inc(deg_ready, 1)

            def inverse_degree(b, i):
                dve.wait_ge(deg_ready, b * T + i + 1)
                nc.vector.reciprocal(rdeg[:, i:i + 1], deg[:, i:i + 1]).then_inc(rdeg_ready, 1)

            def divide(b, i):
                dve.wait_ge(rdeg_ready, b * T + i + 1)
                nc.vector.scalar_tensor_tensor(v[:, i % 2], agg_ps[i % 2][:, 0:F], rdeg[:, i:i + 1], u[:, i],
                                               ALU.mult, ALU.add).then_inc(agg1_free, 1)

            def residual(b, i):
                dve.wait_ge(agg1_free, 2 + b * T + i + 1)
                nc.vector.scalar_tensor_tensor(pre1[:, i % 2], v[:, i % 2], 0.0, x1[:, i],
                                               ALU.max, ALU.add).then_inc(pre1_ready, 1)

            def layer_scales(b):
                dve.wait_ge(row_sum_ready, b * T + FIRST_ROWS)
                if is_first(b):
                    dve.wait_ge(row_mag_ready, 1)
                nc.vector.tensor_scalar(mask[:], row_mag[:], 0.0, None, ALU.is_gt).then_inc(mask_ready, 1)
                nc.vector.tensor_scalar(xk_inv[:], of(inv, OF_X), of(inv, OF_K), 1.0 / Y_DOWN, ALU.mult, ALU.mult).then_inc(xk_inv_ready, 1)
                dve.wait_ge(mask_ready, b + 1)
                nc.vector.tensor_tensor(unmask[:], of(inv, OF_A, T), mask[:], ALU.mult).then_inc(unmask_ready, 1)
                dve.wait_ge(xk_inv_ready, b + 1)
                dve.wait_ge(unmask_ready, b + 1)
                nc.vector.tensor_scalar(agg_inv[:], unmask[:], xk_inv[:], None, ALU.mult).then_inc(agg_inv_ready, 1)

            def split_z(b, i):
                dve.wait_ge(zh_ready, b * T + i + 1)
                nc.vector.scalar_tensor_tensor(z_l[:, i], uz_ps[i % 2][:, F:2 * F], Z_DOWN, z_h[:, i, 0:F],
                                               ALU.mult, ALU.subtract).then_inc(zl_ready, 1)

            def body(b, more):
                for i in range(T):
                    sums(b, 0, i)
                    variance(b, 0, i)
                    if i >= 3:
                        split_z(b, i - 3)
                    inverse_root(b, 0, i)
                    norm(b, 0, i)
                    if i == 0:
                        nc.vector.tensor_scalar(deg_least[:], of(scale, OF_A, T), deg_qe[:], None, ALU.mult).then_inc(deg_least_ready, 1)
                    if i + AHEAD < T:
                        split_adj(b, i + AHEAD)
                    if more and X_FROM <= i < X_FROM + 2 * FT:
                        magnitude_x(b + 1, i - X_FROM)
                    if more and i == X_FROM + 2 * FT - 1:
                        join_magnitude_x(b + 1)
                if more:
                    scales(BEFORE + b, OF_X, 1 + T)
                split_z(b, T - 3)
                if more:
                    split_x(b + 1, 0)
                split_z(b, T - 2)
                split_z(b, T - 1)
                for i in range(T):
                    degree(b, i)
                    if i:
                        variance(b, 1, i - 1)
                    inverse_degree(b, i)
                    if more:
                        for t in PROJECTS[i - 1] if i else ():
                            split_y(b + 1, t)
                    divide(b, i)
                    if i:
                        inverse_root(b, 1, i - 1)
                    residual(b, i)
                    sums(b, 1, i)
                    if i:
                        norm(b, 1, i - 1)
                    elif more:
                        split_x(b + 1, 1)
                    if more and i == T - 2:
                        layer_scales(b + 1)
                    if more and i in SPLITS:
                        split_adj(b + 1, SPLITS[i])
                variance(b, 1, T - 1)
                inverse_root(b, 1, T - 1)
                norm(b, 1, T - 1)

            dve.wait_ge(k_loaded, 16)
            nc.vector.tensor_reduce(of(mag, OF_K), k_in[:], AX.XY, ALU.max, apply_absolute_value=True).then_inc(k_mag_ready, 1)
            scales(OF_K_CHAIN, OF_K)
            for q in range(2 * FT - 1):
                magnitude_x(0, q)
            dve.wait_ge(xt_quarter_ready, 1)
            join_magnitude_x(0)
            dve.wait_ge(kwh_ready, 1)
            nc.vector.scalar_tensor_tensor(k_l[:], k_in[:], k_s, k_h[:], ALU.mult, ALU.subtract).then_inc(kwl_ready, 1)
            scales(OF_X_CHAIN, OF_X)
            magnitude_first(1)
            split_x(0, 0)
            split_x(0, 1)
            split_y(0, 0)
            scales(LOW_CHAIN, OF_A, HALF)
            split_y(0, 1)
            magnitude_first(4)
            split_y(0, 2)
            split_adj(0, 0)
            split_y(0, 3)
            magnitude_first(6)
            split_y(0, 4)
            split_y(0, 5)
            magnitude_first(7)
            split_y(0, 6)
            split_y(0, 7)
            split_adj(0, 1)
            scales(HIGH_CHAIN, OF_A + HALF, HALF)
            dve.wait_ge(x_loaded, 16)
            nc.vector.tensor_reduce(row_mag[:, FIRST_ROWS:T], x_in[:, FIRST_ROWS:T], AX.X, ALU.max,
                                    apply_absolute_value=True).then_inc(row_mag_ready, 1)
            layer_scales(0)
            scales(OF_W_CHAIN, OF_W)
            split_adj(0, 2)
            dve.wait_ge(scale_ready, OF_W_CHAIN + 1)
            nc.vector.tensor_scalar(deg_q[:], w_s, Z_DOWN, None, ALU.mult).then_inc(deg_q_ready, 1)
            nc.vector.tensor_scalar(deg_qe[:], w_s, Z_DOWN * DEG_EPS, None, ALU.mult).then_inc(deg_q_ready, 1)
            dve.wait_ge(kwh_ready, 2)
            nc.vector.scalar_tensor_tensor(w_l[:], w_in[:], w_s, w_h[:], ALU.mult, ALU.subtract).then_inc(kwl_ready, 1)
            dve.wait_ge(deg_q_ready, 2)
            with dve.Fori(0, B - 1) as b:
                body(b, True)
            body(B - 1, False)


def kernel(x, adj, L0_gnn_kernel, L1_gnn_W):
    import numpy as np
    import concourse.bacc as bacc
    from concourse.bass_utils import run_bass_kernel_spmd

    x, adj, k0, w1 = (np.asarray(a) for a in (x, adj, L0_gnn_kernel, L1_gnn_W))
    B, N, F = x.shape
    T, FT = N // P, F // P
    arrays = {
        "adjt": adj.reshape(B, T, P, T, P).transpose(0, 1, 4, 3, 2).reshape(B, T, P, T * P),
        "x": x.reshape(B, T, P, F).transpose(0, 2, 1, 3),
        "xt": x.reshape(B, N, FT, P).transpose(0, 3, 2, 1),
        "k0": k0.reshape(FT, P, F).transpose(1, 0, 2),
        "w1": w1.reshape(F, 2, FT, P).transpose(3, 2, 1, 0).reshape(P, FT, 2 * F),
    }
    arrays = {n: np.ascontiguousarray(a) for n, a in arrays.items()}
    nc = bacc.Bacc("TRN2", target_bir_lowering=False, num_devices=1)
    aps = {n: nc.dram_tensor(n, a.shape, mybir.dt.from_np(a.dtype), kind="ExternalInput").ap() for n, a in arrays.items()}
    out = nc.dram_tensor("out", (B, P, T, F), mybir.dt.float32, kind="ExternalOutput").ap()
    graph_layers(nc, aps["adjt"], aps["x"], aps["xt"], aps["k0"], aps["w1"], out)
    result = run_bass_kernel_spmd(nc, [arrays], core_ids=[0]).results[0]["out"]
    return np.ascontiguousarray(result.transpose(0, 2, 1, 3)).reshape(B, N, F)
```
